# Optimizing a Trainium2 kernel written in Bass

```python
import numpy as np
import jax
import jax.numpy as jnp

def _softmax(x, axis=-1):
    return jax.nn.softmax(x, axis=axis)

def _gelu(x):
    return jax.nn.gelu(x, approximate=True)

def _silu(x):
    return jax.nn.silu(x)

def _sigmoid(x):
    return jax.nn.sigmoid(x)

def _layernorm(x, axis=-1, eps=1e-05):
    m = jnp.mean(x, axis=axis, keepdims=True)
    v = jnp.var(x, axis=axis, keepdims=True)
    return (x - m) / jnp.sqrt(v + eps)

def _scatter_add(tgt, idx, src, axis=0):
    return tgt.at[idx].add(src)

def _segment_sum(src, seg, n):
    return jax.ops.segment_sum(src, seg, n)
kernel_name = 'mk_adj_preln_d2_adj_r2_2f3a7f'

def setup_inputs(seed: int=0):
    np.random.seed(seed)
    _w = jnp.asarray

    def _rec_inputs():
        import jax
        import jax.numpy as jnp
        _gk = jax.random.key(seed)
        x = -2.603e-05 + 0.05003 * jax.random.normal(jax.random.fold_in(_gk, 1), (4096, 128), jnp.float32)
        _a = jax.random.bernoulli(jax.random.fold_in(_gk, 2), 0.000976562, (4096, 4096))
        _a = jnp.logical_or(_a, jnp.swapaxes(_a, -1, -2))
        _a = jnp.logical_or(_a, jnp.eye(4096, dtype=bool))
        _af = _a.astype(jnp.float32)
        _af = _af / jnp.maximum(_af.sum(-1, keepdims=True), 1.0)
        adj = _af
        return (x, adj)
    x, adj = _rec_inputs()

    def _L0_gnn_setup():
        import jax, jax.numpy as jnp
        import numpy as np
        MIN_NORM = 1e-15
        BALL_EPS = 1e-05
        C_IN = 1.0
        C_OUT = 1.0

        def _artanh(x):
            x = jnp.clip(x, -1.0 + 1e-07, 1.0 - 1e-07)
            return 0.5 * (jnp.log1p(x) - jnp.log1p(-x))

        def _norm(x):
            return jnp.maximum(jnp.linalg.norm(x, axis=-1, keepdims=True), MIN_NORM)

        def proj(x, c):
            norm = _norm(x)
            maxnorm = (1.0 - BALL_EPS) / jnp.sqrt(c)
            return jnp.where(norm > maxnorm, x / norm * maxnorm, x)

        def expmap0(u, c):
            sc = jnp.sqrt(c)
            un = _norm(u)
            return jnp.tanh(sc * un) * u / (sc * un)

        def logmap0(p, c):
            sc = jnp.sqrt(c)
            pn = _norm(p)
            return _artanh(sc * pn) * p / (sc * pn)

        def mobius_matvec(m, x, c):
            sc = jnp.sqrt(c)
            xn = _norm(x)
            mx = x @ m.T
            mxn = _norm(mx)
            res = jnp.tanh(mxn / xn * _artanh(sc * xn)) * mx / (mxn * sc)
            zero_row = jnp.all(mx == 0, axis=-1, keepdims=True)
            return jnp.where(zero_row, jnp.zeros((), dtype=res.dtype), res)

        def mobius_add(x, y, c):
            x2 = jnp.sum(x * x, axis=-1, keepdims=True)
            y2 = jnp.sum(y * y, axis=-1, keepdims=True)
            xy = jnp.sum(x * y, axis=-1, keepdims=True)
            num = (1.0 + 2.0 * c * xy + c * y2) * x + (1.0 - c * x2) * y
            denom = 1.0 + 2.0 * c * xy + c * c * x2 * y2
            return num / jnp.maximum(denom, MIN_NORM)
        key = jax.random.key(seed)
        k1, k2, k3, k4 = jax.random.split(key, 4)
        N, D_IN, D_OUT = (4096, 128, 128)
        x = proj(0.05 * jax.random.normal(k1, (N, D_IN), dtype=jnp.float32), C_IN)
        adj = jax.random.uniform(k2, (N, N), dtype=jnp.float32)
        adj = adj / jnp.sum(adj, axis=1, keepdims=True)
        bound = np.sqrt(2.0) * np.sqrt(6.0 / (D_IN + D_OUT))
        weight = jax.random.uniform(k3, (D_OUT, D_IN), dtype=jnp.float32, minval=-bound, maxval=bound)
        bias = 0.01 * jax.random.normal(k4, (D_OUT,), dtype=jnp.float32)
        return {'x': x, 'adj': adj, 'weight': weight, 'bias': bias}
    _L0_gnn_all = _L0_gnn_setup()
    _L0_gnn_in = {k: v for k, v in _L0_gnn_all.items() if k in ('weight', 'bias')}
    del _L0_gnn_all

    def _L1_gnn_setup():
        import jax, jax.numpy as jnp
        import numpy as np
        N = 5000
        NFEAT = 128
        NHID = 128
        key = jax.random.key(seed)
        k1, k2, k3, k4 = jax.random.split(key, 4)
        x = jax.random.normal(k1, (N, NFEAT), dtype=jnp.float32)
        adj = jax.random.uniform(k2, (N, N), dtype=jnp.float32)
        stdv = 1.0 / np.sqrt(NHID)
        weight = jax.random.uniform(k3, (2 * NFEAT, NHID), dtype=jnp.float32, minval=-stdv, maxval=stdv)
        bias = jax.random.uniform(k4, (NHID,), dtype=jnp.float32, minval=-stdv, maxval=stdv)
        return {'x': x, 'adj': adj, 'weight': weight, 'bias': bias}
    _L1_gnn_all = _L1_gnn_setup()
    _L1_gnn_in = {k: v for k, v in _L1_gnn_all.items() if k in ('weight', 'bias')}
    del _L1_gnn_all
    return {'x': x, 'adj': adj, 'L0_gnn_weight': _L0_gnn_in['weight'], 'L0_gnn_bias': _L0_gnn_in['bias'], 'L1_gnn_weight': _L1_gnn_in['weight'], 'L1_gnn_bias': _L1_gnn_in['bias']}

def reference(x, adj, L0_gnn_weight, L0_gnn_bias, L1_gnn_weight, L1_gnn_bias):
    import jax
    import jax.numpy as jnp

    def _L0_gnn_ref(x, adj, weight, bias):
        import jax, jax.numpy as jnp
        import numpy as np
        MIN_NORM = 1e-15
        BALL_EPS = 1e-05
        C_IN = 1.0
        C_OUT = 1.0

        def _artanh(x):
            x = jnp.clip(x, -1.0 + 1e-07, 1.0 - 1e-07)
            return 0.5 * (jnp.log1p(x) - jnp.log1p(-x))

        def _norm(x):
            return jnp.maximum(jnp.linalg.norm(x, axis=-1, keepdims=True), MIN_NORM)

        def proj(x, c):
            norm = _norm(x)
            maxnorm = (1.0 - BALL_EPS) / jnp.sqrt(c)
            return jnp.where(norm > maxnorm, x / norm * maxnorm, x)

        def expmap0(u, c):
            sc = jnp.sqrt(c)
            un = _norm(u)
            return jnp.tanh(sc * un) * u / (sc * un)

        def logmap0(p, c):
            sc = jnp.sqrt(c)
            pn = _norm(p)
            return _artanh(sc * pn) * p / (sc * pn)

        def mobius_matvec(m, x, c):
            sc = jnp.sqrt(c)
            xn = _norm(x)
            mx = x @ m.T
            mxn = _norm(mx)
            res = jnp.tanh(mxn / xn * _artanh(sc * xn)) * mx / (mxn * sc)
            zero_row = jnp.all(mx == 0, axis=-1, keepdims=True)
            return jnp.where(zero_row, jnp.zeros((), dtype=res.dtype), res)

        def mobius_add(x, y, c):
            x2 = jnp.sum(x * x, axis=-1, keepdims=True)
            y2 = jnp.sum(y * y, axis=-1, keepdims=True)
            xy = jnp.sum(x * y, axis=-1, keepdims=True)
            num = (1.0 + 2.0 * c * xy + c * y2) * x + (1.0 - c * x2) * y
            denom = 1.0 + 2.0 * c * xy + c * c * x2 * y2
            return num / jnp.maximum(denom, MIN_NORM)
        h = proj(mobius_matvec(weight, x, C_IN), C_IN)
        hyp_bias = proj(expmap0(bias[None, :], C_IN), C_IN)
        h = proj(mobius_add(h, hyp_bias, C_IN), C_IN)
        x_tangent = logmap0(h, C_IN)
        support_t = adj @ x_tangent
        h = proj(expmap0(support_t, C_IN), C_IN)
        xt = jax.nn.relu(logmap0(h, C_IN))
        return proj(expmap0(xt, C_OUT), C_OUT)

    def _L1_gnn_ref(x, adj, weight, bias):
        import jax, jax.numpy as jnp
        import numpy as np
        N = 5000
        NFEAT = 128
        NHID = 128
        support = adj @ x
        support = jnp.concatenate([x, support], axis=1)
        out = support @ weight + bias
        return jax.nn.relu(out)
    h = jnp.maximum(_layernorm(x, axis=-1), 0.0)
    x = x + _L0_gnn_ref(h, adj, L0_gnn_weight, L0_gnn_bias)
    h = jnp.maximum(_layernorm(x, axis=-1), 0.0)
    x = x + _L1_gnn_ref(h, adj, L1_gnn_weight, L1_gnn_bias)
    return x

_drawn_inputs = setup_inputs


def setup_inputs(seed=0):
    import zlib

    import numpy as np

    out = dict(_drawn_inputs(seed))
    spreads = {}
    factors = {}
    for name, (base, spread) in spreads.items():
        noise = np.random.default_rng([zlib.crc32(name.encode()), seed]).standard_normal(out[name].shape)
        drawn = base * np.exp(spread * noise) if base else spread * noise
        out[name] = jnp.asarray(drawn.astype(out[name].dtype))
    for name, factor in factors.items():
        out[name] = (out[name] * factor).astype(out[name].dtype)
    return out
```

```python
from contextlib import ExitStack

import numpy as np

import concourse.bass as bass
from concourse import mybir

F32 = mybir.dt.float32
F32R = mybir.dt.float32r
I32 = mybir.dt.int32
ACT = mybir.ActivationFunctionType
ALU = mybir.AluOpType
AX_X = mybir.AxisListType.X

P = 128
N = 4096
D = 128
TILES = N // P
BLOCK = 1024
BLOCKS = N // BLOCK
BT = BLOCK // P
PAIRS = TILES // 2
BANK = 512
HALVES = BLOCK // BANK
UNIT = 2 * BLOCK
SLOTS = 8
HI_BUFS, LO_BUFS = 4, 4
LAYER_UNITS = BLOCKS * PAIRS

LN_EPS = 1e-5
MIN_NORM = 1e-15
BALL = float(np.float32(1.0 - 1e-5))
ATANH_CLIP = float(np.float32(1.0 - 1e-7))
ATANH_BALL = float(0.5 * (np.log1p(np.float64(np.float32(BALL))) - np.log1p(-np.float64(np.float32(BALL)))))
SERIES_BELOW = 0.3
SERIES = [1.0 / (2 * k + 1) for k in range(1, 8)]

KEPT_ORDER = [8, 9, 10, 11, 0, 1, 2, 3, 4, 5, 6, 7, 12, 13, 14, 15]
PLAIN_ORDER = list(range(PAIRS))
KEPT_LOADS = list(range(0, 8))

W0T, W0, W1_SELF, W1_AGG, EYE, CENTER, CONSTS = range(7)


def two_layers(nc, x, x_t, adj_units, consts, bias0, bias1, out):
    with ExitStack() as ctx:
        def sb(name, shape, dt=F32):
            return ctx.enter_context(nc.sbuf_tensor(name, shape, dt))

        def sem(name):
            return ctx.enter_context(nc.semaphore(name))

        ring = sb("ring", [P, SLOTS, UNIT])
        adj_hi = sb("adj_hi", [P, HI_BUFS, UNIT], F32R)
        adj_lo = sb("adj_lo", [P, LO_BUFS, UNIT], F32R)
        x_rows = sb("x_rows", [P, TILES, D])
        h_rows = sb("h_rows", [P, TILES, D])
        feat_hi = sb("feat_hi", [P, TILES, D], F32R)
        feat_lo = sb("feat_lo", [P, TILES, D], F32R)
        tmp_a = sb("tmp_a", [P, BT, D])
        tmp_b = sb("tmp_b", [P, BT, D])
        tmp_c = sb("tmp_c", [P, BT, D])
        cst = sb("cst", [P, CONSTS, D])
        b0_col = sb("b0_col", [P, 1])
        b0_row = sb("b0_row", [P, D])
        b1_row = sb("b1_row", [P, D])
        ones = sb("ones", [P, P])
        b0_sq = sb("b0_sq", [P, 1])
        v_col = sb("v_col", [P, 1])
        bs = sb("bs", [P, 8])
        bn6 = sb("bn6", [P, TILES, 6])
        mv = sb("mv", [P, TILES, 2])
        S = 40
        sc = sb("sc", [P, S, TILES])
        root_tmp = sb("root_tmp", [P, 3, TILES])
        ps_ = sb("ps_", [P, 16, BT])
        half_b = sb("half_b", [P, 2, BT])
        mhalf_b = sb("mhalf_b", [P, BT])

        psum = ctx.enter_context(nc.psum_tensor("psum", [P, 8, BANK], F32))
        turned = psum[:, 4:6, :].rearrange("p a b -> p (a b)")
        prod = psum[:, 6:8, :].rearrange("p a b -> p (a b)")

        const_loaded = sem("const_loaded")
        xt_loaded = [sem(f"xt_loaded{c}") for c in range(BLOCKS)]
        x_loaded = sem("x_loaded")
        slot_loaded = [sem(f"slot_loaded{s}") for s in range(SLOTS)]
        made = sem("made")
        setup_v = sem("setup_v")
        setup_p = sem("setup_p")
        setup_g = sem("setup_g")
        setup_a = sem("setup_a")
        centered = sem("centered")
        relued = sem("relued")
        squared = sem("squared")
        projected = sem("projected")
        kept = sem("kept")
        reduced = sem("reduced")
        row_v = sem("row_v")
        row_a = sem("row_a")
        tangent = sem("tangent")
        feat_hi_ready = sem("feat_hi_ready")
        feat_lo_ready = sem("feat_lo_ready")
        hi_ready = sem("hi_ready")
        lo_ready = sem("lo_ready")
        unit_done = sem("unit_done")
        acc_read = sem("acc_read")
        turn_done = sem("turn_done")
        post_a = sem("post_a")
        post_v = sem("post_v")
        post_g = sem("post_g")
        last_v = sem("last_v")
        last_a = sem("last_a")
        last_p = sem("last_p")
        stored = sem("stored")

        ident = cst[:, EYE, :]

        def ring_pair(slot):
            return ring[:, slot, :]

        xt_sb = ring[:, 6:8, :].rearrange("p a b -> p (a b)")
        ut = [ring[:, 5, i * BLOCK:(i + 1) * BLOCK] for i in range(2)]
        ut_sq = [ring[:, 4, i * BLOCK:(i + 1) * BLOCK] for i in range(2)]
        mx_sq = [tmp_a, tmp_b]
        cen = psum[:, 0:2, :].rearrange("p a b -> p (a b)")
        u_norm2 = psum[:, 2, 0:TILES]
        mx_dot_b = psum[:, 3, 0:TILES]
        setup_ps = psum[:, 0, 0:2]

        block = ctx.enter_context(nc.Block())

        @block.sync
        def _(sp):
            sp.dma_start(cst[:, :, :], consts).then_inc(const_loaded, 16)
            sp.dma_start(b0_col[:, :], bias0.rearrange("(d a) -> d a", a=1)).then_inc(const_loaded, 16)
            sp.dma_start(b0_row[:, :], bias0.rearrange("(a d) -> a d", a=1).broadcast_to([P, D])).then_inc(const_loaded, 16)
            sp.dma_start(b1_row[:, :], bias1.rearrange("(a d) -> a d", a=1).broadcast_to([P, D])).then_inc(const_loaded, 16)
            for c in range(BLOCKS):
                sp.dma_start(xt_sb[:, c * BLOCK:(c + 1) * BLOCK], x_t[:, c * BLOCK:(c + 1) * BLOCK]).then_inc(xt_loaded[c], 16)
            sp.dma_start(x_rows[:, :, :], x.rearrange("(t p) d -> p t d", p=P)).then_inc(x_loaded, 16)

            def load(slot, unit):
                sp.dma_start(ring_pair(slot), adj_units[unit]).then_inc(slot_loaded[slot], 16)

            for u in range(4):
                load(u, u)
            sp.wait_ge(projected, BLOCKS)
            for u in range(4, SLOTS):
                load(u, u)
            for u in range(SLOTS, PAIRS):
                sp.wait_ge(lo_ready, u - SLOTS + 1)
                load(u % SLOTS, u)
            with sp.Fori(1, BLOCKS) as b:
                for u in range(PAIRS):
                    sp.wait_ge(lo_ready, b * PAIRS + (u - SLOTS + 1))
                    load(u % SLOTS, b * PAIRS + u)
            for k in KEPT_LOADS:
                sp.wait_ge(lo_ready, LAYER_UNITS + k % 4 + 1 + 4 * (k // 4))
                load(k % 4, (BLOCKS - 1) * PAIRS + k)
            with sp.Fori(1, BLOCKS) as b:
                for u in range(PAIRS):
                    sp.wait_ge(lo_ready, b * PAIRS + (LAYER_UNITS + u - SLOTS + 1))
                    load(u % SLOTS, b * (-PAIRS) + ((BLOCKS - 1) * PAIRS + u))

        @block.gpsimd
        def _(pool):
            nc.gpsimd.memset(ones[:, :], 1.0).then_inc(made, 1)
            nc.gpsimd.memset(half_b[:, :, :], 0.5).then_inc(made, 1)
            nc.gpsimd.memset(mhalf_b[:, :], -0.5).then_inc(made, 1)
            pool.wait_ge(made, 3)
            pool.wait_ge(setup_v, 3)
            nc.gpsimd.tensor_tensor(bs[:, 1:2], bs[:, 0:1], half_b[:, 0, 0:1], ALU.pow).then_inc(setup_g, 1)
            with pool.Fori(1, BLOCKS + 1) as b:
                pool.wait_ge(post_v, (b - 1) * POST_V + POSTV["sums"])
                nc.gpsimd.tensor_tensor(ps_[:, 2:4, :], ps_[:, 0:2, :], half_b[:, :, :], ALU.pow).then_inc(post_g, 1)
                pool.wait_ge(post_v, (b - 1) * POST_V + POSTV["var"])
                nc.gpsimd.tensor_tensor(ps_[:, 12, :], ps_[:, 11, :], mhalf_b[:, :], ALU.pow).then_inc(post_g, 1)

        @block.tensor
        def _(pe):
            pe.wait_ge(const_loaded, 64)
            pe.wait_ge(made, 3)
            pe.wait_ge(setup_v, 1)
            nc.tensor.matmul(setup_ps[:, 0:1], cst[:, W0, :], b0_col[:, :], start=True, stop=True)
            nc.tensor.matmul(setup_ps[:, 1:2], ones[:, :], b0_sq[:, :], start=True, stop=True).then_inc(setup_p, 1)
            pe.wait_ge(setup_v, 3)

            def center(c):
                pe.wait_ge(xt_loaded[c], 16)
                if c:
                    pe.wait_ge(relued, c)
                for h in range(HALVES):
                    q = slice(h * BANK, (h + 1) * BANK)
                    mm = nc.tensor.matmul(cen[:, q], cst[:, CENTER, :], xt_sb[:, c * BLOCK + h * BANK:c * BLOCK + (h + 1) * BANK],
                                          start=True, stop=True)
                mm.then_inc(centered, 1)

            def project(c):
                mx = turned if c % 2 == 0 else prod
                pe.wait_ge(relued, c + 1)
                if c >= 2:
                    pe.wait_ge(kept, 2 * (c - 1))
                for t in range(BT):
                    ut_t = ut[c % 2][:, t * P:(t + 1) * P]
                    nc.tensor.matmul(mx[:, t * D:(t + 1) * D], ut_t, cst[:, W0T, :], start=True, stop=True)
                    n = c * BT + t
                    nc.tensor.matmul(mx_dot_b[:, n:n + 1], ut_t, v_col[:, :], start=True, stop=True)
                pe.wait_ge(squared, c + 1)
                for t in range(BT):
                    n = c * BT + t
                    mm = nc.tensor.matmul(u_norm2[:, n:n + 1], ut_sq[c % 2][:, t * P:(t + 1) * P], ones[:, 0:1], start=True, stop=True)
                mm.then_inc(projected, 1)

            center(0)
            for c in range(BLOCKS):
                if c + 1 < BLOCKS:
                    center(c + 1)
                project(c)

            def multiply(n0, b, order, feat_waits, hooks):
                acc0 = (b % 2) * HALVES
                for u, k in enumerate(order):
                    if u in hooks:
                        hooks[u]()
                    if k in feat_waits:
                        pe.wait_ge(feat_hi_ready, feat_waits[k])
                        pe.wait_ge(feat_lo_ready, feat_waits[k])
                    hb, lb = u % HI_BUFS, u % LO_BUFS
                    for part, ready, buf in (("hi", hi_ready, adj_hi[:, hb, :]), ("lo", lo_ready, adj_lo[:, lb, :])):
                        pe.wait_ge(ready, n0 + u + 1)
                        for e in range(2):
                            for w in ((feat_hi, feat_lo) if part == "hi" else (feat_hi,)):
                                for h in range(HALVES):
                                    mm = nc.tensor.matmul(psum[:, acc0 + h, :], w[:, 2 * k + e, :],
                                                          buf[:, e * BLOCK + h * BANK:e * BLOCK + (h + 1) * BANK],
                                                          start=(u == 0 and part == "hi" and e == 0 and w is feat_hi),
                                                          stop=(u == PAIRS - 1 and part == "lo" and e == 1))
                    mm.then_inc(unit_done, 1)

            def turn(src, waits):
                for s, v in waits:
                    pe.wait_ge(s, v)
                for t in range(BT):
                    mm = nc.tensor.transpose(turned[:, t * P:(t + 1) * P], src[:, t, :], ident)
                mm.then_inc(turn_done, 1)

            pe.wait_ge(kept, 2 * BLOCKS)
            pe.wait_ge(row_v, ROW["sums"])
            multiply(0, 0, PLAIN_ORDER, {0: 1, 4: 2, 8: 3, 12: 4}, {})
            with pe.Fori(1, BLOCKS) as b:
                multiply(b * PAIRS, b, PLAIN_ORDER, {}, {
                    1: lambda: turn(tmp_a, [(acc_read, b)])})
            multiply(LAYER_UNITS, 0, KEPT_ORDER, {8: BLOCKS + 1, 0: BLOCKS + 2, 4: BLOCKS + 3, 12: BLOCKS + 4}, {
                1: lambda: turn(tmp_a, [(acc_read, BLOCKS)])})

            def last_products(n):
                pe.wait_ge(last_a, 2 * n)
                for t in range(BT):
                    nc.tensor.matmul(prod[:, t * D:(t + 1) * D], tmp_b[:, t, :], cst[:, W1_SELF, :], start=True, stop=False)
                    mm = nc.tensor.matmul(prod[:, t * D:(t + 1) * D], tmp_a[:, t, :], cst[:, W1_AGG, :], start=False, stop=True)
                mm.then_inc(last_p, 1)

            with pe.Fori(1, BLOCKS) as b:
                multiply(b * PAIRS + LAYER_UNITS, b, PLAIN_ORDER, {}, {
                    1: lambda: turn(tmp_c, [(last_v, (b - 1) * LAST_V + LASTV["h"])]),
                    3: lambda: last_products(b)})
            turn(tmp_c, [(last_v, (BLOCKS - 1) * LAST_V + LASTV["h"])])
            last_products(BLOCKS)

        @block.scalar
        def _(act):
            act.wait_ge(setup_v, 4)
            nc.scalar.activation(bs[:, 3:4], bs[:, 2:3], ACT.Tanh).then_inc(setup_a, 1)
            for c in range(BLOCKS + 1):
                if c < BLOCKS:
                    act.wait_ge(centered, c + 1)
                    if c >= 2:
                        act.wait_ge(projected, c - 1)
                    nc.scalar.activation(ut[c % 2], cen, ACT.Relu).then_inc(relued, 1)
                    act.wait_ge(relued, c + 1)
                    nc.scalar.activation(ut_sq[c % 2], ut[c % 2], ACT.Square).then_inc(squared, 1)
                if c:
                    k = c - 1
                    mx = turned if k % 2 == 0 else prod
                    act.wait_ge(projected, k + 1)
                    nc.scalar.activation(h_rows[:, k * BT:(k + 1) * BT, :].rearrange("p t d -> p (t d)"), mx, ACT.Copy).then_inc(kept, 1)
                    if k >= 2:
                        act.wait_ge(reduced, k - 1)
                    nc.scalar.activation(mx_sq[k % 2][:, :, :].rearrange("p t d -> p (t d)"), mx, ACT.Square).then_inc(kept, 1)
            act.wait_ge(row_v, ROW["ln1_in"])
            nc.scalar.activation(sc[:, 9, :], sc[:, 8, :], ACT.Ln).then_inc(row_a, 1)
            act.wait_ge(row_v, ROW["tanh_in"])
            nc.scalar.activation(sc[:, 11, :], sc[:, 10, :], ACT.Tanh).then_inc(row_a, 1)
            act.wait_ge(row_v, ROW["ln2_in"])
            nc.scalar.activation(sc[:, 13, :], sc[:, 12, :], ACT.Ln).then_inc(row_a, 1)

            def split_hi(n, u, slot, loads, first=False):
                if loads is not None:
                    act.wait_ge(slot_loaded[slot], loads * 16)
                if not first:
                    act.wait_ge(unit_done, n - HI_BUFS + 1)
                nc.scalar.activation(adj_hi[:, u % HI_BUFS, :], ring_pair(slot), ACT.Copy).then_inc(hi_ready, 1)

            def copy_acc(count_before, dst, b):
                act.wait_ge(unit_done, count_before)
                acc = psum[:, ((b - 1) % 2) * HALVES:((b - 1) % 2) * HALVES + HALVES, :] if isinstance(b, int) else \
                    psum[:, bass.ds(((b + 1) % 2) * HALVES, HALVES), :]
                return nc.scalar.activation(dst[:, :, :].rearrange("p t d -> p (t d)"), acc.rearrange("p a b -> p (a b)"), ACT.Copy)

            for u, k in enumerate(PLAIN_ORDER):
                if u % 4 == 0:
                    c = u // 4
                    rows = slice(c * BT, (c + 1) * BT)
                    act.wait_ge(tangent, c + 1)
                    nc.scalar.activation(feat_hi[:, rows, :], h_rows[:, rows, :], ACT.Copy).then_inc(feat_hi_ready, 1)
                split_hi(u, u, u % SLOTS, u // SLOTS + 1, first=u < HI_BUFS)
            nc.scalar.activation(bs[:, 7:8], bs[:, 2:3], ACT.Tanh).then_inc(setup_a, 1)

            def post(b, step):
                base = (b - 1) * POST_A
                if step == 0:
                    i = copy_acc(b * PAIRS, tmp_a, b)
                    i.then_inc(acc_read, 1)
                elif step == 1:
                    act.wait_ge(turn_done, b)
                    nc.scalar.activation(tmp_b[:, :, :].rearrange("p t d -> p (t d)"), turned, ACT.Square).then_inc(post_a, 1)
                elif step == 2:
                    nc.scalar.activation(tmp_c[:, :, :].rearrange("p t d -> p (t d)"), turned, ACT.Relu).then_inc(post_a, 1)
                elif step == 3:
                    act.wait_ge(post_a, base + 2)
                    nc.scalar.activation(tmp_a[:, :, :].rearrange("p t d -> p (t d)"),
                                         tmp_c[:, :, :].rearrange("p t d -> p (t d)"), ACT.Square).then_inc(post_a, 1)
                elif step == 4:
                    act.wait_ge(post_v, (b - 1) * POST_V + POSTV["tanh_in"])
                    nc.scalar.activation(ps_[:, 8, :], ps_[:, 7, :], ACT.Tanh).then_inc(post_a, 1)

            POST_AT = {3: [0], 5: [1], 6: [2, 3], 11: [4]}
            with act.Fori(1, BLOCKS) as b:
                for u in range(PAIRS):
                    for step in POST_AT.get(u, []):
                        post(b, step)
                    split_hi(b * PAIRS + u, u, u % SLOTS, b * 2 + (u // SLOTS + 1))

            def feat_split(c, count):
                rows = slice(c * BT, (c + 1) * BT)
                nc.scalar.activation(feat_hi[:, rows, :], h_rows[:, rows, :], ACT.Relu).then_inc(feat_hi_ready, 1)

            PRE = 2 * BLOCKS
            for u, k in enumerate(KEPT_ORDER):
                n = LAYER_UNITS + u
                if u == 0:
                    act.wait_ge(unit_done, LAYER_UNITS - 4)
                    act.wait_ge(post_v, (BLOCKS - 2) * POST_V + POSTV["h"])
                    feat_split(2, 1)
                if u == 1:
                    feat_split(0, 2)
                if u == 2:
                    feat_split(1, 3)
                for step in {3: [0], 5: [1], 6: [2, 3], 9: [4]}.get(u, []):
                    post(BLOCKS, step)
                slot = k % SLOTS if k >= 8 else k % 4
                loads = PRE if k >= 8 else PRE + 1 + k // 4
                split_hi(n, u, slot, loads)
                if u == 13:
                    act.wait_ge(post_v, (BLOCKS - 1) * POST_V + POSTV["h"])
                    feat_split(3, 4)

            def last(b, step):
                if step == 0:
                    copy_acc(b * PAIRS + LAYER_UNITS, tmp_a, b).then_inc(last_a, 1)
                elif step == 1:
                    act.wait_ge(turn_done, b + BLOCKS)
                    nc.scalar.activation(tmp_b[:, :, :].rearrange("p t d -> p (t d)"), turned, ACT.Copy).then_inc(last_a, 1)
                else:
                    act.wait_ge(last_v, (b - 1) * LAST_V + LASTV["y"])
                    act.dma_start(out_blocks[b * -1 + BLOCKS], tmp_c[:, :, :]).then_inc(stored, 16)

            out_blocks = out.rearrange("(g t p) d -> g p t d", p=P, t=BT)
            LAST_AT = {3: 0, 5: 1, 11: 2}
            with act.Fori(1, BLOCKS) as b:
                for u in range(PAIRS):
                    if u in LAST_AT:
                        last(b, LAST_AT[u])
                    slot = u % SLOTS
                    loads = PRE + 2 + u // SLOTS + 1 if slot < 4 else PRE + u // SLOTS + 1
                    split_hi(b * PAIRS + (LAYER_UNITS + u), u, slot, (b - 1) * 2 + loads)
            for step in range(3):
                last(BLOCKS, step)
            act.wait_ge(stored, 16 * BLOCKS)

        @block.vector
        def _(dve):
            V = nc.vector

            def steps(s, names):
                state = {"n": 0}

                def done(ins, name=None):
                    ins.then_inc(s, 1)
                    state["n"] += 1
                    if name:
                        assert names[name] == state["n"], (name, state["n"])
                    return state["n"]
                return done

            dve.wait_ge(const_loaded, 64)
            V.tensor_tensor(b0_sq[:, :], b0_col[:, :], b0_col[:, :], ALU.mult).then_inc(setup_v, 1)
            dve.wait_ge(setup_p, 1)
            V.tensor_copy(v_col[:, :], setup_ps[:, 0:1]).then_inc(setup_v, 1)
            V.tensor_copy(bs[:, 0:1], setup_ps[:, 1:2]).then_inc(setup_v, 1)
            dve.wait_ge(setup_g, 1)
            V.tensor_scalar(bs[:, 2:3], bs[:, 1:2], MIN_NORM, None, ALU.max).then_inc(setup_v, 1)
            dve.wait_ge(setup_a, 1)
            V.tensor_scalar(bs[:, 4:5], bs[:, 3:4], BALL, None, ALU.min).then_inc(setup_v, 1)
            dve.wait_ge(setup_v, 5)
            V.reciprocal(bs[:, 5:6], bs[:, 2:3]).then_inc(setup_v, 1)
            V.tensor_tensor(bs[:, 6:7], bs[:, 4:5], bs[:, 4:5], ALU.mult).then_inc(setup_v, 1)
            dve.wait_ge(setup_v, 6)
            V.tensor_tensor(bs[:, 0:1], bs[:, 4:5], bs[:, 5:6], ALU.mult).then_inc(setup_v, 1)
            cb, y2 = bs[:, 0:1], bs[:, 6:7]
            dve.wait_ge(setup_v, 8)

            done = steps(row_v, ROW)
            dve.wait_ge(x_loaded, 16)
            for t in range(TILES):
                i = V.bn_stats(bn6[:, t, :], x_rows[:, t, :])
            done(i, "bn")
            dve.wait_ge(row_v, ROW["bn"])
            for t in range(TILES):
                i = V.bn_aggr(mv[:, t, :], bn6[:, t, :])
            done(i, "aggr")
            for c in range(BLOCKS):
                dve.wait_ge(kept, 2 * (c + 1))
                V.tensor_reduce(sc[:, 2, c * BT:(c + 1) * BT], mx_sq[c % 2][:, :, :], AX_X, ALU.add).then_inc(reduced, 1)
            dve.wait_ge(row_v, ROW["aggr"])
            V.tensor_scalar(sc[:, 0, :], mv[:, :, 1], LN_EPS, None, ALU.add)
            dve.wait_ge(projected, BLOCKS)
            V.tensor_copy(sc[:, 1, :], u_norm2)
            MB = sc[:, 14, :]
            dve.wait_ge(reduced, BLOCKS)
            done(V.tensor_copy(MB, mx_dot_b), "sums")

            def r(i):
                return sc[:, i, :]

            def need(n):
                dve.wait_ge(row_v, n)

            def artanh(w, ratio, t, ln_name, ln_out, ln_count):
                done(V.tensor_scalar(r(t), r(w), -1.0, 1.0, ALU.mult, ALU.add))
                n = done(V.tensor_tensor(r(t + 3), r(w), r(w), ALU.mult))
                need(n)
                n = done(V.reciprocal(r(t + 1), r(t)))
                need(n)
                done(V.scalar_tensor_tensor(out=r(ratio), in0=r(w), scalar=1.0, in1=r(t + 1), op0=ALU.add, op1=ALU.mult), ln_name)
                n = done(V.tensor_scalar(r(t + 2), r(t + 3), SERIES[-1], None, ALU.mult))
                for co in SERIES[-2::-1]:
                    need(n)
                    n = done(V.scalar_tensor_tensor(out=r(t + 2), in0=r(t + 2), scalar=co, in1=r(t + 3), op0=ALU.add, op1=ALU.mult))
                need(n)
                done(V.tensor_scalar(r(t + 1), r(w), SERIES_BELOW, None, ALU.is_ge))
                n = done(V.scalar_tensor_tensor(out=r(t + 3), in0=r(t + 2), scalar=1.0, in1=r(w), op0=ALU.add, op1=ALU.mult))
                need(n)
                dve.wait_ge(row_a, ln_count)
                n = done(V.scalar_tensor_tensor(out=r(t), in0=r(ln_out), scalar=0.5, in1=r(t + 3), op0=ALU.mult, op1=ALU.subtract))
                need(n)
                n = done(V.tensor_tensor(r(t + 2), r(t), r(t + 1), ALU.mult))
                need(n)
                n = done(V.tensor_tensor(r(t + 4), r(t + 2), r(t + 3), ALU.add))
                need(n)

            def root(v, out_inv, out_root, shape):
                y, a = out_inv, root_tmp[:, 0:shape, :]
                i = done(V.tensor_scalar(a.bitcast(I32), v.bitcast(I32), 1, None, ALU.logical_shift_right))
                need(i)
                i = done(V.tensor_scalar(y.bitcast(I32), a.bitcast(I32), -1, 0x5F3759DF, ALU.mult, ALU.add))
                for _ in range(3):
                    need(i)
                    i = done(V.scalar_tensor_tensor(out=a, in0=y, scalar=-0.5, in1=v, op0=ALU.mult, op1=ALU.mult))
                    need(i)
                    i = done(V.tensor_tensor(a, a, y, ALU.mult))
                    need(i)
                    i = done(V.scalar_tensor_tensor(out=y, in0=a, scalar=1.5, in1=y, op0=ALU.add, op1=ALU.mult))
                need(i)
                if out_root is not None:
                    done(V.tensor_tensor(out_root[0], out_root[1], out_root[2], ALU.mult), out_root[3])

            need(ROW["sums"])
            root(sc[:, 0:3, :], sc[:, 3:6, :], (sc[:, 4:6, :], sc[:, 1:3, :], sc[:, 4:6, :], "roots"), 3)
            need(ROW["roots"])
            RSTD, UN, MN_ = r(3), r(4), r(5)
            done(V.tensor_tensor(r(15), UN, RSTD, ALU.mult))
            n = done(V.tensor_tensor(r(16), MN_, RSTD, ALU.mult))
            need(n)
            done(V.tensor_scalar(r(17), r(15), MIN_NORM, None, ALU.max))
            done(V.tensor_scalar(r(18), r(16), MIN_NORM, None, ALU.max))
            n = done(V.tensor_scalar(r(19), r(15), MIN_NORM, ATANH_CLIP, ALU.max, ALU.min))
            need(n)
            done(V.reciprocal(r(20), r(17)))
            n = done(V.reciprocal(r(21), r(18)))
            need(n)
            done(V.tensor_tensor(r(22), r(18), r(20), ALU.mult))
            artanh(19, 8, 23, "ln1_in", 9, 1)
            done(V.tensor_tensor(r(10), r(22), r(27), ALU.mult), "tanh_in")
            n = done(V.tensor_tensor(r(28), RSTD, r(21), ALU.mult))
            need(n)
            n = done(V.tensor_tensor(r(29), r(28), MB, ALU.mult))
            dve.wait_ge(row_a, 2)
            n = done(V.tensor_scalar(r(30), r(11), BALL, None, ALU.min))
            need(n)
            PN = r(30)
            done(V.tensor_tensor(r(31), PN, PN, ALU.mult))
            done(V.scalar_tensor_tensor(out=r(15), in0=r(29), scalar=cb, in1=PN, op0=ALU.mult, op1=ALU.mult))
            n = done(V.tensor_tensor(r(32), r(28), PN, ALU.mult))
            need(n)
            done(V.tensor_scalar(r(16), r(15), 2.0, 1.0, ALU.mult, ALU.add))
            n = done(V.tensor_scalar(r(17), r(31), -1.0, 1.0, ALU.mult, ALU.add))
            need(n)
            done(V.tensor_scalar(r(18), r(16), y2, None, ALU.add))
            n = done(V.scalar_tensor_tensor(out=r(20), in0=r(31), scalar=y2, in1=r(16), op0=ALU.mult, op1=ALU.add))
            need(n)
            n = done(V.tensor_scalar(r(21), r(20), MIN_NORM, None, ALU.max))
            need(n)
            n = done(V.reciprocal(r(22), r(21)))
            need(n)
            done(V.tensor_tensor(r(33), r(18), r(22), ALU.mult))
            n = done(V.tensor_tensor(r(34), r(17), r(22), ALU.mult))
            need(n)
            done(V.tensor_tensor(r(35), r(33), PN, ALU.mult))
            done(V.tensor_tensor(r(36), r(33), r(34), ALU.mult))
            done(V.tensor_scalar(r(37), r(34), y2, None, ALU.mult))
            n = done(V.tensor_scalar(r(38), r(15), 2.0, None, ALU.mult))
            need(n)
            done(V.tensor_tensor(r(16), r(35), r(35), ALU.mult))
            done(V.tensor_tensor(r(17), r(36), r(38), ALU.mult))
            n = done(V.tensor_tensor(r(18), r(37), r(34), ALU.mult))
            need(n)
            n = done(V.tensor_tensor(r(20), r(16), r(17), ALU.add))
            need(n)
            n = done(V.tensor_tensor(r(21), r(20), r(18), ALU.add))
            need(n)
            done(V.tensor_scalar(r(6), r(21), 0.0, None, ALU.max), "zn2")
            need(ROW["zn2"])
            root(sc[:, 6:7, :], sc[:, 15:16, :], (sc[:, 7, :], sc[:, 6, :], sc[:, 15, :], "zn"), 1)
            need(ROW["zn"])
            done(V.tensor_scalar(r(39), r(7), MIN_NORM, None, ALU.max))
            n = done(V.tensor_scalar(r(19), r(7), MIN_NORM, BALL, ALU.max, ALU.min))
            need(n)
            n = done(V.reciprocal(r(20), r(39)))
            artanh(19, 12, 23, "ln2_in", 13, 3)
            n = done(V.tensor_tensor(r(21), r(27), r(20), ALU.mult))
            need(n)
            done(V.tensor_tensor(r(22), r(21), r(33), ALU.mult))
            n = done(V.tensor_tensor(r(35), r(21), r(34), ALU.mult))
            need(n)
            done(V.tensor_tensor(r(36), r(22), r(32), ALU.mult))
            n = done(V.tensor_scalar(r(37), r(35), cb, None, ALU.mult))
            need(n)

            def split_lo(n, u, slot, first=False):
                dve.wait_ge(hi_ready, n + 1)
                if not first:
                    dve.wait_ge(unit_done, n - LO_BUFS + 1)
                V.tensor_tensor(adj_lo[:, u % LO_BUFS, :], ring_pair(slot), adj_hi[:, u % HI_BUFS, :].bitcast(F32),
                                ALU.subtract).then_inc(lo_ready, 1)

            bias_part = [tmp_a, tmp_b]

            def tangent_of(c):
                rows = slice(c * BT, (c + 1) * BT)
                V.tensor_tensor(bias_part[c % 2][:, :, :], b0_row[:, None, :].broadcast_to([P, BT, D]),
                                r(37)[:, rows, None].broadcast_to([P, BT, D]), ALU.mult).then_inc(row_v, 1)
                need(ROW_END + c + 1)
                for t in range(BT):
                    j = c * BT + t
                    i = V.scalar_tensor_tensor(out=h_rows[:, j, :], in0=h_rows[:, j, :], scalar=sc[:, 36, j:j + 1],
                                               in1=bias_part[c % 2][:, t, :], op0=ALU.mult, op1=ALU.add)
                i.then_inc(tangent, 1)

            def tangent_lo(c):
                rows = slice(c * BT, (c + 1) * BT)
                dve.wait_ge(feat_hi_ready, c + 1)
                V.tensor_tensor(feat_lo[:, rows, :], h_rows[:, rows, :], feat_hi[:, rows, :].bitcast(F32),
                                ALU.subtract).then_inc(feat_lo_ready, 1)

            ROW_END = n
            assert ROW_END == ROW["end"], ROW_END
            tangent_of(0)
            tangent_lo(0)
            for u in range(PAIRS):
                split_lo(u, u, u % SLOTS, first=u < LO_BUFS)
                if u % 4 == 0 and u // 4 + 1 < BLOCKS:
                    tangent_of(u // 4 + 1)
                if u % 4 == 3 and u // 4 + 1 < BLOCKS:
                    tangent_lo(u // 4 + 1)

            def post(b, step):
                v0, a0, g0 = (b - 1) * POST_V, (b - 1) * POST_A, (b - 1) * 2
                t0 = (b - 1) * BT
                q = lambda i: ps_[:, i, :]

                def did(ins, name):
                    ins.then_inc(post_v, 1)

                if step == 0:
                    dve.wait_ge(post_a, a0 + 1)
                    did(V.tensor_reduce(q(0), tmp_b[:, :, :], AX_X, ALU.add), "s2")
                elif step == 1:
                    dve.wait_ge(post_a, a0 + 3)
                    did(V.tensor_reduce(q(1), tmp_a[:, :, :], AX_X, ALU.add), "sums")
                elif step == 2:
                    dve.wait_ge(post_g, g0 + 1)
                    did(V.tensor_scalar(q(4), q(2), MIN_NORM, None, ALU.max), "un")
                    did(V.tensor_scalar(q(5), q(2), ATANH_BALL, None, ALU.min), "clipped")
                    dve.wait_ge(post_v, v0 + 4)
                    did(V.reciprocal(q(6), q(4)), "run")
                    dve.wait_ge(post_v, v0 + 5)
                    did(V.tensor_tensor(q(9), q(5), q(6), ALU.mult), "c1")
                    dve.wait_ge(post_v, v0 + 6)
                    did(V.tensor_tensor(q(10), q(9), q(3), ALU.mult), "rn0")
                    dve.wait_ge(post_v, v0 + 7)
                    did(V.tensor_scalar(q(7), q(10), MIN_NORM, None, ALU.max), "tanh_in")
                elif step == 3:
                    dve.wait_ge(post_v, v0 + 8)
                    did(V.reciprocal(q(13), q(7)), "rrn")
                    dve.wait_ge(post_v, v0 + 9)
                    did(V.tensor_tensor(q(14), q(13), q(9), ALU.mult), "c2")
                    dve.wait_ge(post_v, v0 + 10)
                    dve.wait_ge(post_a, a0 + 4)
                    did(V.scalar_tensor_tensor(out=q(15), in0=q(8), scalar=BALL, in1=q(14), op0=ALU.min, op1=ALU.mult), "c")
                    dve.wait_ge(post_v, v0 + 11)
                    for t in range(BT):
                        i = V.scalar_tensor_tensor(out=x_rows[:, t0 + t, :], in0=tmp_c[:, t, :], scalar=ps_[:, 15, t:t + 1],
                                                   in1=x_rows[:, t0 + t, :], op0=ALU.mult, op1=ALU.add)
                    did(i, "x1")
                elif step == 4:
                    for t in range(BT):
                        i = V.bn_stats(bn6[:, t, :], x_rows[:, t0 + t, :])
                    did(i, "bn")
                elif step == 5:
                    for t in range(BT):
                        i = V.bn_aggr(mv[:, t, :], bn6[:, t, :])
                    did(i, "aggr")
                    dve.wait_ge(post_v, v0 + 14)
                    did(V.tensor_scalar(q(11), mv[:, 0:BT, 1], LN_EPS, None, ALU.add), "var")
                elif step == 6:
                    dve.wait_ge(post_g, g0 + 2)
                    for t in range(BT):
                        i = V.tensor_scalar(h_rows[:, t0 + t, :], x_rows[:, t0 + t, :], mv[:, t, 0:1], ps_[:, 12, t:t + 1],
                                            ALU.subtract, ALU.mult)
                    did(i, "h")

            def before_post(b, step):
                if step in (4, 5):
                    dve.wait_ge(post_v, (b - 1) * POST_V + {4: 12, 5: 13}[step])

            POST_AT = {5: 0, 6: 1, 8: 2, 11: 3, 12: 4, 13: 5, 15: 6}
            with dve.Fori(1, BLOCKS) as b:
                for u in range(PAIRS):
                    before_post(b, POST_AT.get(u))
                    split_lo(b * PAIRS + u, u, u % SLOTS)
                    if u in POST_AT:
                        post(b, POST_AT[u])

            def feat_split(c, count):
                rows = slice(c * BT, (c + 1) * BT)
                dve.wait_ge(feat_hi_ready, BLOCKS + count)
                V.scalar_tensor_tensor(out=feat_lo[:, rows, :].rearrange("p t d -> p (t d)"),
                                       in0=h_rows[:, rows, :].rearrange("p t d -> p (t d)"), scalar=0.0,
                                       in1=feat_hi[:, rows, :].bitcast(F32).rearrange("p t d -> p (t d)"),
                                       op0=ALU.max, op1=ALU.subtract).then_inc(feat_lo_ready, 1)

            for u, k in enumerate(KEPT_ORDER):
                if u == 0:
                    feat_split(2, 1)
                if u == 1:
                    feat_split(0, 2)
                if u == 2:
                    feat_split(1, 3)
                slot = k % SLOTS if k >= 8 else k % 4
                before_post(BLOCKS, KEPT_POST_AT.get(u))
                split_lo(LAYER_UNITS + u, u, slot)
                if u in KEPT_POST_AT:
                    post(BLOCKS, KEPT_POST_AT[u])
                if u == 13:
                    feat_split(3, 4)

            def last(b, step):
                v0 = (b - 1) * LAST_V
                rows = bass.ds(b * -BT + TILES, BT) if not isinstance(b, int) else slice(TILES - b * BT, TILES - b * BT + BT)
                if step == 0:
                    V.tensor_scalar(tmp_c[:, :, :], h_rows[:, rows, :], 0.0, None, ALU.max).then_inc(last_v, 1)
                else:
                    dve.wait_ge(last_p, b)
                    V.tensor_tensor(tmp_c[:, :, :], prod.rearrange("p (t d) -> p t d", d=D),
                                    b1_row[:, None, :].broadcast_to([P, BT, D]), ALU.add).then_inc(last_v, 1)
                    dve.wait_ge(last_v, v0 + 2)
                    V.scalar_tensor_tensor(out=tmp_c[:, :, :].rearrange("p t d -> p (t d)"),
                                           in0=tmp_c[:, :, :].rearrange("p t d -> p (t d)"), scalar=0.0,
                                           in1=x_rows[:, rows, :].rearrange("p t d -> p (t d)"),
                                           op0=ALU.max, op1=ALU.add).then_inc(last_v, 1)

            with dve.Fori(1, BLOCKS) as b:
                for u in range(PAIRS):
                    split_lo(b * PAIRS + (LAYER_UNITS + u), u, u % SLOTS)
                    if u == 0:
                        last(b, 0)
                    if u == 8:
                        last(b, 1)
                dve.wait_ge(stored, b * 16)
            last(BLOCKS, 0)
            last(BLOCKS, 1)


ROW = {"bn": 1, "aggr": 2, "sums": 3, "roots": 15, "ln1_in": 27, "tanh_in": 40, "zn2": 64, "zn": 76, "ln2_in": 83, "end": 100}
POSTV = {"sums": 2, "tanh_in": 8, "var": 15, "h": 16}
POST_V, POST_A = 16, 4
LASTV = {"h": 1, "y": 3}
LAST_V = 3
KEPT_POST_AT = {5: 0, 6: 1, 8: 2, 9: 3, 10: 4, 11: 5, 12: 6}


def kernel(x, adj, L0_gnn_weight, L0_gnn_bias, L1_gnn_weight, L1_gnn_bias):
    import concourse.bacc as bacc
    from concourse.bass_utils import run_bass_kernel_spmd

    x, adj, w0, w1 = (np.ascontiguousarray(a) for a in (x, adj, L0_gnn_weight, L1_gnn_weight))
    units = adj.reshape(BLOCKS, BLOCK, PAIRS, 2, P).transpose(0, 2, 4, 3, 1)
    units = np.ascontiguousarray(units).reshape(LAYER_UNITS, P, UNIT)
    eye = np.eye(D, dtype=np.float32)
    center = eye - np.float32(1.0 / D)
    consts = np.ascontiguousarray(np.stack([w0.T, w0, w1[:D], w1[D:], eye, center], axis=1))
    arrays = {
        "x": x, "x_t": np.ascontiguousarray(x.T), "adj_units": units, "consts": consts,
        "bias0": np.ascontiguousarray(L0_gnn_bias), "bias1": np.ascontiguousarray(L1_gnn_bias),
    }
    nc = bacc.Bacc("TRN2", target_bir_lowering=False, num_devices=1, dynamic_dma_scratch_size=1024)
    args = [nc.dram_tensor(k, a.shape, mybir.dt.from_np(a.dtype), kind="ExternalInput").ap() for k, a in arrays.items()]
    args.append(nc.dram_tensor("out", (N, D), F32, kind="ExternalOutput").ap())
    two_layers(nc, *args)
    got = run_bass_kernel_spmd(nc, [arrays], core_ids=[0])
    return got.results[0]["out"]
```

```python
from contextlib import ExitStack

import numpy as np

import concourse.bass as bass
from concourse import mybir

F32 = mybir.dt.float32
F32R = mybir.dt.float32r
I32 = mybir.dt.int32
ACT = mybir.ActivationFunctionType
ALU = mybir.AluOpType
AX_X = mybir.AxisListType.X

P = 128
N = 4096
D = 128
TILES = N // P
BLOCK = 1024
BLOCKS = N // BLOCK
BT = BLOCK // P
PAIRS = TILES // 2
BANK = 512
HALVES = BLOCK // BANK
HALF = BT // 2
UNIT = 2 * BLOCK
SLOTS = 8
HI_BUFS, LO_BUFS = 4, 4
LAYER_UNITS = BLOCKS * PAIRS
PLAIN = 4
assert PLAIN % HI_BUFS == 0 and PLAIN % LO_BUFS == 0 and PLAIN <= SLOTS

LN_EPS = 1e-5
MIN_NORM = 1e-15
BALL = float(np.float32(1.0 - 1e-5))
ATANH_CLIP = float(np.float32(1.0 - 1e-7))
ATANH_BALL = float(0.5 * (np.log1p(np.float64(np.float32(BALL))) - np.log1p(-np.float64(np.float32(BALL)))))
BALL_RQ = float(1.0 / ((1.0 - np.float64(np.float32(BALL))) * (1.0 + np.float64(np.float32(BALL)))))
SERIES_BELOW = 0.15
SERIES = [1.0 / (2 * k + 1) for k in range(1, 4)]

ORDER0 = list(range(PAIRS // 2, PAIRS)) + list(range(PAIRS // 2))
ORDER1 = list(range(PAIRS))
assert SLOTS == PAIRS // 2

W0T, W0, W1_SELF, W1_AGG, EYE, CENTER, CONSTS = range(7)


def two_layers(nc, x, x_t, adj_units, consts, bias0, bias1, out):
    with ExitStack() as ctx:
        def sb(name, shape, dt=F32):
            return ctx.enter_context(nc.sbuf_tensor(name, shape, dt))

        def sem(name):
            return ctx.enter_context(nc.semaphore(name))

        ring = sb("ring", [P, SLOTS, UNIT])
        adj_hi = sb("adj_hi", [P, HI_BUFS, UNIT], F32R)
        adj_lo = sb("adj_lo", [P, LO_BUFS, UNIT], F32R)
        x_rows = sb("x_rows", [P, TILES, D])
        h_rows = sb("h_rows", [P, TILES, D])
        feat_hi = sb("feat_hi", [P, TILES, D], F32R)
        feat_lo = sb("feat_lo", [P, TILES, D], F32R)
        tmp_a = sb("tmp_a", [P, BT, D])
        tmp_b = sb("tmp_b", [P, BT, D])
        tmp_c = sb("tmp_c", [P, BT, D])
        cst = sb("cst", [P, CONSTS, D])
        b0_col = sb("b0_col", [P, 1])
        b0_row = sb("b0_row", [P, D])
        b1_row = sb("b1_row", [P, D])
        ones = sb("ones", [P, P])
        b0_sq = sb("b0_sq", [P, 1])
        w0t_v = sb("w0t_v", [P, D + 1])
        bs = sb("bs", [P, 11])
        bn6 = sb("bn6", [P, TILES, 6])
        mv = sb("mv", [P, TILES, 2])
        sc = sb("sc", [P, 40, TILES])
        row_sums = sb("row_sums", [P, TILES, 2])
        root_tmp = sb("root_tmp", [P, 6, TILES])
        ps_ = sb("ps_", [P, 16, BT])
        half_b = sb("half_b", [P, 2, BT])
        mhalf_b = sb("mhalf_b", [P, BT])

        psum = ctx.enter_context(nc.psum_tensor("psum", [P, 8, BANK], F32))
        turned = psum[:, 4:6, :].rearrange("p a b -> p (a b)")
        prod = psum[:, 6:8, :].rearrange("p a b -> p (a b)")

        const_loaded = sem("const_loaded")
        xt_loaded = [sem(f"xt_loaded{c}") for c in range(BLOCKS)]
        x_loaded = [sem(f"x_loaded{c}") for c in range(BLOCKS)]
        slot_loaded = [sem(f"slot_loaded{s}") for s in range(SLOTS)]
        made = sem("made")
        setup_v = sem("setup_v")
        setup_p = sem("setup_p")
        setup_g = sem("setup_g")
        setup_a = sem("setup_a")
        centered = sem("centered")
        relued = sem("relued")
        squared = sem("squared")
        projected = sem("projected")
        kept = sem("kept")
        reduced = sem("reduced")
        row_v = sem("row_v")
        row_a = sem("row_a")
        tangent = sem("tangent")
        feat_hi_ready = sem("feat_hi_ready")
        feat_lo_ready = sem("feat_lo_ready")
        hi_ready = sem("hi_ready")
        lo_ready = sem("lo_ready")
        unit_done = sem("unit_done")
        acc_read = sem("acc_read")
        turn_done = sem("turn_done")
        post_a = sem("post_a")
        post_v = sem("post_v")
        post_g = sem("post_g")
        last_v = sem("last_v")
        last_a = sem("last_a")
        last_p = sem("last_p")
        stored = sem("stored")

        ident = cst[:, EYE, :]

        rstd = sc[:, 3, :]
        (w1, ratio1, log1, stretched, tanh_arg, tanh_out, unit, xy_p, pn, x2, xy_2, gain, A, B, den, Ap, xB, BB,
         rden, rq) = (sc[:, 14 + i, :] for i in range(20))
        alpha, beta, num, over, inv = w1, log1, stretched, tanh_arg, xB
        zn, w2_, zm, rz, ratio2, log2, shrunk = tanh_out, unit, xy_p, pn, x2, xy_2, gain

        def ring_pair(slot):
            return ring[:, slot, :]

        xt_sb = ring[:, 6:8, :].rearrange("p a b -> p (a b)")
        ut = [ring[:, 5, i * BLOCK:(i + 1) * BLOCK] for i in range(2)]
        ut_sq = [ring[:, 4, i * BLOCK:(i + 1) * BLOCK] for i in range(2)]
        mx_sq = [buf[:, i * HALF:(i + 1) * HALF, :] for buf in (tmp_a, tmp_b) for i in range(2)]
        MX_SQ_BUFS = len(mx_sq)
        cen = [psum[:, 2 * i:2 * i + 2, :].rearrange("p a b -> p (a b)") for i in range(2)]
        mx_all = psum[:, 4:8, :].rearrange("p a (i c) -> p (a i) c", c=2 * D)
        setup_ps = psum[:, 0, 0:2]

        block = ctx.enter_context(nc.Block())

        @block.sync
        def _(sp):
            x_tiles = x.rearrange("(t p) d -> p t d", p=P)
            sp.dma_start(cst[:, :, :], consts).then_inc(const_loaded, 16)
            sp.dma_start(b0_col[:, :], bias0.rearrange("(d a) -> d a", a=1)).then_inc(const_loaded, 16)
            sp.dma_start(b0_row[:, :], bias0.rearrange("(a d) -> a d", a=1).broadcast_to([P, D])).then_inc(const_loaded, 16)
            sp.dma_start(b1_row[:, :], bias1.rearrange("(a d) -> a d", a=1).broadcast_to([P, D])).then_inc(const_loaded, 16)
            for c in range(BLOCKS):
                sp.dma_start(xt_sb[:, c * BLOCK:(c + 1) * BLOCK], x_t[:, c * BLOCK:(c + 1) * BLOCK]).then_inc(xt_loaded[c], 16)
                sp.dma_start(x_rows[:, c * BT:(c + 1) * BT, :], x_tiles[:, c * BT:(c + 1) * BT, :]).then_inc(x_loaded[c], 16)

            def load(slot, unit):
                sp.dma_start(ring_pair(slot), adj_units[unit]).then_inc(slot_loaded[slot], 16)

            for u in range(4):
                load(u, ORDER0[u])
            sp.wait_ge(projected, 2 * BLOCKS)
            for u in range(4, SLOTS):
                load(u, ORDER0[u])
            for u in range(SLOTS, PAIRS):
                if u - SLOTS < PLAIN:
                    sp.wait_ge(unit_done, u - SLOTS + 1)
                else:
                    sp.wait_ge(lo_ready, u - SLOTS + 1 - PLAIN)
                load(u % SLOTS, ORDER0[u])
            with sp.Fori(1, BLOCKS) as b:
                for u in range(PAIRS):
                    sp.wait_ge(lo_ready, b * PAIRS + (u - SLOTS + 1 - PLAIN))
                    load(u % SLOTS, b * PAIRS + ORDER0[u])
            for u in range(SLOTS, PAIRS):
                sp.wait_ge(lo_ready, LAYER_UNITS + u - SLOTS + 1 - PLAIN)
                load(u % SLOTS, (BLOCKS - 1) * PAIRS + u)
            with sp.Fori(1, BLOCKS) as b:
                for u in range(PAIRS):
                    sp.wait_ge(lo_ready, b * PAIRS + (LAYER_UNITS + u - SLOTS + 1 - PLAIN))
                    load(u % SLOTS, b * (-PAIRS) + ((BLOCKS - 1) * PAIRS + u))

        @block.gpsimd
        def _(pool):
            nc.gpsimd.memset(ones[:, :], 1.0).then_inc(made, 1)
            nc.gpsimd.memset(half_b[:, :, :], 0.5).then_inc(made, 1)
            nc.gpsimd.memset(mhalf_b[:, :], -0.5).then_inc(made, 1)
            pool.wait_ge(made, 3)
            pool.wait_ge(setup_v, 3)
            nc.gpsimd.tensor_tensor(bs[:, 1:2], bs[:, 0:1], half_b[:, 0, 0:1], ALU.pow).then_inc(setup_g, 1)
            with pool.Fori(1, BLOCKS + 1) as b:
                pool.wait_ge(post_a, (b - 1) * POST_A + POSTA["sums"])
                nc.gpsimd.tensor_tensor(ps_[:, 2:4, :], ps_[:, 0:2, :], half_b[:, :, :], ALU.pow).then_inc(post_g, 1)
                pool.wait_ge(post_v, (b - 1) * POST_V + POSTV["var"])
                nc.gpsimd.tensor_tensor(ps_[:, 12, :], ps_[:, 11, :], mhalf_b[:, :], ALU.pow).then_inc(post_g, 1)

        @block.tensor
        def _(pe):
            def warm_up(count):
                for _ in range(count):
                    nc.tensor.matmul(turned[:, 0:P], ones[:, :], ones[:, :], start=True, stop=True)

            pe.wait_ge(made, 3)
            warm_up(8)
            pe.wait_ge(const_loaded, 64)
            pe.wait_ge(setup_v, 1)
            nc.tensor.matmul(setup_ps[:, 0:1], cst[:, W0, :], b0_col[:, :], start=True, stop=True)
            nc.tensor.matmul(setup_ps[:, 1:2], ones[:, :], b0_sq[:, :], start=True, stop=True).then_inc(setup_p, 1)
            pe.wait_ge(setup_v, 3)

            def center(c):
                pe.wait_ge(xt_loaded[c], 16)
                if c >= 2:
                    pe.wait_ge(relued, c - 1)
                for h in range(HALVES):
                    q = slice(h * BANK, (h + 1) * BANK)
                    mm = nc.tensor.matmul(cen[c % 2][:, q], cst[:, CENTER, :], xt_sb[:, c * BLOCK + h * BANK:c * BLOCK + (h + 1) * BANK],
                                          start=True, stop=True)
                mm.then_inc(centered, 1)

            def project(m):
                c, first = m // 2, m % 2 * HALF
                if m == 0:
                    pe.wait_ge(setup_v, 3)
                if m % 2 == 0:
                    pe.wait_ge(relued, c + 1)
                if m >= 2:
                    pe.wait_ge(kept, 3 * (m - 2) + 2)
                for t in range(first, first + HALF):
                    nc.tensor.matmul(mx_all[:, t, 0:D + 1], ut[c % 2][:, t * P:(t + 1) * P], w0t_v[:, :], start=True, stop=True)
                if m % 2 == 0:
                    pe.wait_ge(squared, c + 1)
                for t in range(first, first + HALF):
                    mm = nc.tensor.matmul(mx_all[:, t, D + 1:D + 2], ut_sq[c % 2][:, t * P:(t + 1) * P], ones[:, 0:1], start=True, stop=True)
                mm.then_inc(projected, 1)

            center(0)
            for c in range(BLOCKS):
                project_at = [2 * c, 2 * c + 1]
                if c + 1 < BLOCKS:
                    center(c + 1)
                for m in project_at:
                    project(m)

            def multiply(n0, b, order, feat_waits, hooks, plain=0):
                acc0 = (b % 2) * HALVES
                for u, k in enumerate(order):
                    if u in hooks:
                        hooks[u]()
                    if u < plain and 2 * k in [first for first, _ in GROUPS]:
                        pe.wait_ge(tangent, [first for first, _ in GROUPS].index(2 * k) + 1)
                    if k in feat_waits:
                        pe.wait_ge(feat_hi_ready, feat_waits[k])
                        pe.wait_ge(feat_lo_ready, feat_waits[k])
                    if u < plain:
                        pe.wait_ge(slot_loaded[u], 16)
                        for e in range(2):
                            for h in range(HALVES):
                                mm = nc.tensor.matmul(psum[:, acc0 + h, :], h_rows[:, 2 * k + e, :],
                                                      ring[:, u, e * BLOCK + h * BANK:e * BLOCK + (h + 1) * BANK],
                                                      start=(u == 0 and e == 0), stop=False)
                        mm.then_inc(unit_done, 1)
                        continue
                    hb, lb = u % HI_BUFS, u % LO_BUFS
                    for part, ready, buf in (("hi", hi_ready, adj_hi[:, hb, :]), ("lo", lo_ready, adj_lo[:, lb, :])):
                        pe.wait_ge(ready, n0 + (u + 1 - PLAIN))
                        for e in range(2):
                            for w in ((feat_hi, feat_lo) if part == "hi" else (feat_hi,)):
                                for h in range(HALVES):
                                    mm = nc.tensor.matmul(psum[:, acc0 + h, :], w[:, 2 * k + e, :],
                                                          buf[:, e * BLOCK + h * BANK:e * BLOCK + (h + 1) * BANK],
                                                          start=(plain == 0 and u == 0 and part == "hi" and e == 0 and w is feat_hi),
                                                          stop=(u == PAIRS - 1 and part == "lo" and e == 1))
                    mm.then_inc(unit_done, 1)

            def turn(src, waits):
                for s, v in waits:
                    pe.wait_ge(s, v)
                for t in range(BT):
                    mm = nc.tensor.transpose(turned[:, t * P:(t + 1) * P], src[:, t, :], ident)
                mm.then_inc(turn_done, 1)

            pe.wait_ge(row_v, ROW["ln2_in"])
            warm_up(8)
            pe.wait_ge(kept, 3 * 2 * BLOCKS - 1)
            multiply(0, 0, ORDER0, {first // 2: g + 1 for g, (first, _) in enumerate(FEATS[:-1])}, {}, plain=PLAIN)
            pe.wait_ge(feat_hi_ready, len(FEATS))
            pe.wait_ge(feat_lo_ready, len(FEATS))
            with pe.Fori(1, BLOCKS) as b:
                multiply(b * PAIRS, b, ORDER0, {}, {
                    1: lambda: turn(tmp_a, [(acc_read, b)])})
            multiply(LAYER_UNITS, 0, ORDER1, {c * BT // 2: NG + c + 1 for c in range(BLOCKS)}, {
                1: lambda: turn(tmp_a, [(acc_read, BLOCKS)])})

            def last_products(n):
                pe.wait_ge(last_a, 2 * n)
                for t in range(BT):
                    nc.tensor.matmul(prod[:, t * D:(t + 1) * D], tmp_b[:, t, :], cst[:, W1_SELF, :], start=True, stop=False)
                    mm = nc.tensor.matmul(prod[:, t * D:(t + 1) * D], tmp_a[:, t, :], cst[:, W1_AGG, :], start=False, stop=True)
                mm.then_inc(last_p, 1)

            with pe.Fori(1, BLOCKS) as b:
                multiply(b * PAIRS + LAYER_UNITS, b, ORDER1, {}, {
                    1: lambda: turn(tmp_c, [(last_v, (b - 1) * LAST_V + LASTV["h"])]),
                    3: lambda: last_products(b)})
            turn(tmp_c, [(last_v, (BLOCKS - 1) * LAST_V + LASTV["h"])])
            last_products(BLOCKS)

        @block.scalar
        def _(act):
            def split_hi(n, u, slot, loads, first=False):
                if loads is not None:
                    act.wait_ge(slot_loaded[slot], loads * 16)
                if not first:
                    act.wait_ge(unit_done, n - HI_BUFS + 1)
                nc.scalar.activation(adj_hi[:, u % HI_BUFS, :], ring_pair(slot), ACT.Copy).then_inc(hi_ready, 1)

            act.wait_ge(setup_v, 4)
            nc.scalar.activation(bs[:, 3:4], bs[:, 2:3], ACT.Tanh).then_inc(setup_a, 1)
            for c in range(BLOCKS + 1):
                if c < BLOCKS:
                    act.wait_ge(centered, c + 1)
                    if c >= 2:
                        act.wait_ge(projected, 2 * (c - 1))
                    nc.scalar.activation(ut[c % 2], cen[c % 2], ACT.Relu).then_inc(relued, 1)
                if c:
                    for m in (2 * c - 2, 2 * c - 1):
                        here, tiles = slice(m % 2 * HALF, (m % 2 + 1) * HALF), slice(m * HALF, (m + 1) * HALF)
                        act.wait_ge(projected, m + 1)
                        nc.scalar.activation(h_rows[:, tiles, :], mx_all[:, here, 0:D], ACT.Copy).then_inc(kept, 1)
                        nc.scalar.activation(row_sums[:, tiles, :], mx_all[:, here, D:D + 2], ACT.Copy).then_inc(kept, 1)
                        act.wait_ge(kept, 3 * m + 1)
                        if m >= MX_SQ_BUFS:
                            act.wait_ge(reduced, m - MX_SQ_BUFS + 1)
                        nc.scalar.activation(mx_sq[m % MX_SQ_BUFS], h_rows[:, tiles, :], ACT.Square).then_inc(kept, 1)
            act.wait_ge(row_v, ROW["ln1_in"])
            nc.scalar.activation(log1, ratio1, ACT.Ln).then_inc(row_a, 1)
            act.wait_ge(row_v, ROW["tanh_in"])
            nc.scalar.activation(tanh_out, tanh_arg, ACT.Tanh).then_inc(row_a, 1)
            for u in range(PLAIN, PLAIN + PRE_SPLIT):
                split_hi(u, u, u, 1, first=True)
            act.wait_ge(row_v, ROW["ln2_in"])
            nc.scalar.activation(log2, ratio2, ACT.Ln).then_inc(row_a, 1)

            def copy_acc(count_before, dst, b):
                act.wait_ge(unit_done, count_before)
                acc = psum[:, ((b - 1) % 2) * HALVES:((b - 1) % 2) * HALVES + HALVES, :] if isinstance(b, int) else \
                    psum[:, bass.ds(((b + 1) % 2) * HALVES, HALVES), :]
                return nc.scalar.activation(dst[:, :, :].rearrange("p t d -> p (t d)"), acc.rearrange("p a b -> p (a b)"), ACT.Copy)

            for u in range(PLAIN + PRE_SPLIT, PAIRS + 1):
                if u in FEAT_AT:
                    f = FEAT_AT[u]
                    rows = slice(*FEATS[f])
                    act.wait_ge(tangent, FEAT_TANGENTS[f])
                    nc.scalar.activation(feat_hi[:, rows, :], h_rows[:, rows, :], ACT.Copy).then_inc(feat_hi_ready, 1)
                if u < PAIRS:
                    split_hi(u, u, u % SLOTS, u // SLOTS + 1, first=(u < PLAIN + HI_BUFS))
            nc.scalar.activation(bs[:, 7:8], bs[:, 2:3], ACT.Tanh).then_inc(setup_a, 1)

            def post(b, step):
                base = (b - 1) * POST_A
                if step == 0:
                    i = copy_acc(b * PAIRS, tmp_a, b)
                    i.then_inc(acc_read, 1)
                elif step == 1:
                    act.wait_ge(turn_done, b)
                    for t in range(BT):
                        i = nc.scalar.activation(tmp_b[:, t, :], turned[:, t * D:(t + 1) * D], ACT.Square, accum_out=ps_[:, 0, t:t + 1])
                    i.then_inc(post_a, 1)
                elif step == 2:
                    nc.scalar.activation(tmp_c[:, :, :].rearrange("p t d -> p (t d)"), turned, ACT.Relu).then_inc(post_a, 1)
                elif step == 3:
                    act.wait_ge(post_a, base + 2)
                    for t in range(BT):
                        i = nc.scalar.activation(tmp_b[:, t, :], tmp_c[:, t, :], ACT.Square, accum_out=ps_[:, 1, t:t + 1])
                    i.then_inc(post_a, 1)
                elif step == 4:
                    act.wait_ge(post_v, (b - 1) * POST_V + POSTV["tanh_in"])
                    nc.scalar.activation(ps_[:, 8, :], ps_[:, 7, :], ACT.Tanh).then_inc(post_a, 1)
                elif step == 5:
                    act.wait_ge(post_v, (b - 1) * POST_V + POSTV["shift"])
                    for t in range(BT):
                        tile = (b - 1) * BT + t
                        i = nc.scalar.activation(h_rows[:, tile, :], x_rows[:, tile, :], ACT.Relu,
                                                 bias=ps_[:, 13, t:t + 1], scale=ps_[:, 12, t:t + 1])
                    i.then_inc(post_a, 1)

            POST_AT = {3: 0, 5: 1, 6: 2, 7: 3, 11: 4}

            def layer0_block(b, finish_before):
                for u in range(PAIRS):
                    if u == 1 and finish_before:
                        post(b - 1, 5)
                    if u in POST_AT:
                        post(b, POST_AT[u])
                    split_hi(b * PAIRS + u, u, u % SLOTS, b * 2 + (u // SLOTS + 1))

            layer0_block(1, False)
            with act.Fori(2, BLOCKS) as b:
                layer0_block(b, True)

            def feat_split(c):
                rows = slice(c * BT, (c + 1) * BT)
                act.wait_ge(post_a, (c + 1) * POST_A)
                act.wait_ge(unit_done, LAYER_UNITS - PAIRS + ORDER0.index((c + 1) * BT // 2 - 1) + 1)
                nc.scalar.activation(feat_hi[:, rows, :], h_rows[:, rows, :], ACT.Copy).then_inc(feat_hi_ready, 1)

            PRE = 2 * BLOCKS
            for u in range(PAIRS):
                if u == 1:
                    post(BLOCKS - 1, 5)
                for step in KEPT_POST_ACT.get(u, []):
                    post(BLOCKS, step)
                for c in KEPT_FEAT_ACT.get(u, []):
                    feat_split(c)
                split_hi(LAYER_UNITS + u, u, u % SLOTS, PRE + u // SLOTS)

            def last(b, step):
                if step == 0:
                    copy_acc(b * PAIRS + LAYER_UNITS, tmp_a, b).then_inc(last_a, 1)
                elif step == 1:
                    act.wait_ge(turn_done, b + BLOCKS)
                    nc.scalar.activation(tmp_b[:, :, :].rearrange("p t d -> p (t d)"), turned, ACT.Copy).then_inc(last_a, 1)
                else:
                    act.wait_ge(last_v, (b - 1) * LAST_V + LASTV["y"])
                    act.dma_start(out_blocks[b * -1 + BLOCKS], tmp_c[:, :, :]).then_inc(stored, 16)

            out_blocks = out.rearrange("(g t p) d -> g p t d", p=P, t=BT)
            LAST_AT = {3: 0, 5: 1, 11: 2}
            with act.Fori(1, BLOCKS) as b:
                for u in range(PAIRS):
                    if u in LAST_AT:
                        last(b, LAST_AT[u])
                    split_hi(b * PAIRS + (LAYER_UNITS + u), u, u % SLOTS, b * 2 + (PRE + u // SLOTS))
            for step in range(3):
                last(BLOCKS, step)
            act.wait_ge(stored, 16 * BLOCKS)

        @block.vector
        def _(dve):
            V = nc.vector

            def steps(s, names):
                state = {"n": 0}

                def done(ins, name=None):
                    ins.then_inc(s, 1)
                    state["n"] += 1
                    if name:
                        assert names[name] == state["n"], (name, state["n"])
                    return state["n"]
                return done

            def split_lo(n, u, slot, first=False):
                dve.wait_ge(hi_ready, n + (1 - PLAIN))
                if not first:
                    dve.wait_ge(unit_done, n - LO_BUFS + 1)
                V.tensor_tensor(adj_lo[:, u % LO_BUFS, :], ring_pair(slot), adj_hi[:, u % HI_BUFS, :].bitcast(F32),
                                ALU.subtract).then_inc(lo_ready, 1)

            dve.wait_ge(const_loaded, 64)
            V.tensor_tensor(b0_sq[:, :], b0_col[:, :], b0_col[:, :], ALU.mult).then_inc(setup_v, 1)
            dve.wait_ge(setup_p, 1)
            V.tensor_copy(w0t_v[:, D:D + 1], setup_ps[:, 0:1])
            V.tensor_copy(w0t_v[:, 0:D], cst[:, W0T, :]).then_inc(setup_v, 1)
            V.tensor_copy(bs[:, 0:1], setup_ps[:, 1:2]).then_inc(setup_v, 1)
            dve.wait_ge(setup_g, 1)
            V.tensor_scalar(bs[:, 2:3], bs[:, 1:2], MIN_NORM, None, ALU.max).then_inc(setup_v, 1)
            dve.wait_ge(setup_a, 1)
            V.tensor_scalar(bs[:, 4:5], bs[:, 3:4], BALL, None, ALU.min).then_inc(setup_v, 1)
            dve.wait_ge(setup_v, 5)
            V.reciprocal(bs[:, 5:6], bs[:, 2:3]).then_inc(setup_v, 1)
            V.tensor_tensor(bs[:, 6:7], bs[:, 4:5], bs[:, 4:5], ALU.mult).then_inc(setup_v, 1)
            dve.wait_ge(setup_v, 6)
            V.tensor_tensor(bs[:, 0:1], bs[:, 4:5], bs[:, 5:6], ALU.mult).then_inc(setup_v, 1)
            cb, y2 = bs[:, 0:1], bs[:, 6:7]
            dve.wait_ge(setup_v, 8)
            cb_2, inv_1_y2 = bs[:, 8:9], bs[:, 10:11]
            V.tensor_scalar(cb_2, cb, 2.0, None, ALU.mult).then_inc(setup_v, 1)
            V.tensor_scalar(bs[:, 9:10], y2, -1.0, 1.0, ALU.mult, ALU.add).then_inc(setup_v, 1)
            dve.wait_ge(setup_v, 10)
            V.reciprocal(inv_1_y2, bs[:, 9:10]).then_inc(setup_v, 1)
            dve.wait_ge(setup_v, 11)

            done = steps(row_v, ROW)
            dot_b = row_sums[:, :, 0]
            def square_ut(c):
                dve.wait_ge(relued, c + 1)
                if c >= 2:
                    dve.wait_ge(projected, 2 * (c - 1))
                V.tensor_tensor(ut_sq[c % 2], ut[c % 2], ut[c % 2], ALU.mult).then_inc(squared, 1)

            def aggregate(c):
                dve.wait_ge(row_v, ROW[f"bn{c}"])
                for t in range(c * BT, (c + 1) * BT):
                    i = V.bn_aggr(mv[:, t, :], bn6[:, t, :])
                if c == BLOCKS - 1:
                    done(i, "aggr")
                    dve.wait_ge(row_v, ROW["aggr"])
                    done(V.tensor_scalar(sc[:, 0, :], mv[:, :, 1], LN_EPS, None, ALU.add), "var")

            square_ut(0)
            square_ut(1)
            for c in range(BLOCKS):
                batch = slice(c * BT, (c + 1) * BT)
                dve.wait_ge(x_loaded[c], 16)
                for t in range(c * BT, (c + 1) * BT):
                    i = V.bn_stats(bn6[:, t, :], x_rows[:, t, :])
                done(i, f"bn{c}")
                if c == BLOCKS - 1:
                    aggregate(c)
                for m in (2 * c, 2 * c + 1):
                    dve.wait_ge(kept, 3 * m + 3)
                    V.tensor_reduce(sc[:, 2, m * HALF:(m + 1) * HALF], mx_sq[m % MX_SQ_BUFS], AX_X, ALU.add).then_inc(reduced, 1)
                if c + 2 < BLOCKS:
                    square_ut(c + 2)
                if c < BLOCKS - 1:
                    aggregate(c)
            dve.wait_ge(reduced, 2 * BLOCKS)
            dve.wait_ge(kept, 3 * 2 * BLOCKS)
            done(V.tensor_copy(sc[:, 1, :], row_sums[:, :, 1]), "sums")

            def need(n):
                dve.wait_ge(row_v, n)

            def artanh_times(w, ratio_steps, log, logs, out, tmp, out_name, factor):
                s, w2, wk, wm, hk = (sc[:, tmp + i, :] for i in range(5))
                i_r = ratio_steps[0]()
                i_w2 = done(V.tensor_tensor(w2, w, w, ALU.mult))
                i_hk = done(V.tensor_scalar(hk, w, SERIES_BELOW, 0.5, ALU.is_ge, ALU.mult))
                need(i_r)
                i_r = ratio_steps[1]()
                need(i_w2)
                i_s = done(V.tensor_scalar(s, w2, SERIES[2], None, ALU.mult))
                for step in ratio_steps[2:]:
                    need(i_r)
                    i_r = step()
                k, i_k = factor()
                need(i_s)
                i_s = done(V.scalar_tensor_tensor(out=s, in0=s, scalar=SERIES[1], in1=w2, op0=ALU.add, op1=ALU.mult))
                need(i_k)
                i_wk = done(V.tensor_tensor(wk, w, k, ALU.mult))
                need(i_s)
                i_s = done(V.scalar_tensor_tensor(out=s, in0=s, scalar=SERIES[0], in1=w2, op0=ALU.add, op1=ALU.mult))
                need(max(i_wk, i_hk))
                i_wm = done(V.scalar_tensor_tensor(out=wm, in0=w, scalar=SERIES_BELOW, in1=wk, op0=ALU.is_lt, op1=ALU.mult))
                i_hk = done(V.tensor_tensor(hk, hk, k, ALU.mult))
                need(i_wm)
                i_s = done(V.scalar_tensor_tensor(out=s, in0=s, scalar=1.0, in1=wm, op0=ALU.add, op1=ALU.mult))
                need(i_hk)
                dve.wait_ge(row_a, logs)
                i_l = done(V.tensor_tensor(hk, log, hk, ALU.mult))
                need(i_l)
                return done(V.tensor_tensor(out, hk, s, ALU.add), out_name)

            def root(v, y, a, b):
                i = done(V.tensor_scalar(a.bitcast(I32), v.bitcast(I32), 1, None, ALU.logical_shift_right))
                need(i)
                i = done(V.tensor_scalar(y.bitcast(I32), a.bitcast(I32), -1, 0x5F3759DF, ALU.mult, ALU.add))
                need(i)
                i = done(V.tensor_tensor(a, y, v, ALU.mult))
                need(i)
                i = done(V.tensor_tensor(a, a, y, ALU.mult))
                need(i)
                i = done(V.tensor_scalar(b, a, 0.3755269, -1.2521496, ALU.mult, ALU.add))
                need(i)
                i = done(V.tensor_tensor(b, b, a, ALU.mult))
                need(i)
                i = done(V.scalar_tensor_tensor(out=y, in0=b, scalar=1.8766229, in1=y, op0=ALU.add, op1=ALU.mult))
                need(i)
                i = done(V.scalar_tensor_tensor(out=a, in0=y, scalar=-0.5, in1=v, op0=ALU.mult, op1=ALU.mult))
                need(i)
                i = done(V.tensor_tensor(a, a, y, ALU.mult))
                need(i)
                i = done(V.scalar_tensor_tensor(out=y, in0=a, scalar=1.5, in1=y, op0=ALU.add, op1=ALU.mult))
                need(i)

            need(ROW["sums"])
            root(sc[:, 0:3, :], sc[:, 3:6, :], root_tmp[:, 0:3, :], root_tmp[:, 3:6, :])
            n = done(V.tensor_tensor(sc[:, 6:8, :], sc[:, 4:6, :], sc[:, 1:3, :], ALU.mult))
            need(n)
            n = done(V.tensor_tensor(sc[:, 8:10, :], sc[:, 6:8, :], rstd[:, None, :].broadcast_to([P, 2, TILES]), ALU.mult))
            need(n)
            n = done(V.tensor_scalar(w1, sc[:, 8, :], MIN_NORM, ATANH_CLIP, ALU.max, ALU.min))
            norms = done(V.tensor_scalar(sc[:, 10:12, :], sc[:, 8:10, :], MIN_NORM, None, ALU.max))
            need(n)

            def stretch():
                need(norms)
                n = done(V.reciprocal(sc[:, 12:14, :], sc[:, 10:12, :]))
                need(n)
                return stretched, done(V.tensor_tensor(stretched, sc[:, 11, :], sc[:, 12, :], ALU.mult))

            artanh_times(w1, [
                lambda: done(V.tensor_scalar(ratio1, w1, -1.0, 1.0, ALU.mult, ALU.add)),
                lambda: done(V.reciprocal(ratio1, ratio1)),
                lambda: done(V.scalar_tensor_tensor(out=ratio1, in0=w1, scalar=1.0, in1=ratio1, op0=ALU.add, op1=ALU.mult), "ln1_in"),
            ], log1, 1, tanh_arg, 34, "tanh_in", stretch)
            n = done(V.tensor_tensor(unit, rstd, sc[:, 13, :], ALU.mult))
            need(n)
            done(V.scalar_tensor_tensor(out=xy_p, in0=unit, scalar=cb_2, in1=dot_b, op0=ALU.mult, op1=ALU.mult))
            dve.wait_ge(row_a, 2)
            n = done(V.tensor_scalar(pn, tanh_out, BALL, None, ALU.min))
            need(n)
            done(V.tensor_tensor(x2, pn, pn, ALU.mult))
            n = done(V.tensor_tensor(xy_2, xy_p, pn, ALU.mult))
            n_g = done(V.tensor_tensor(gain, unit, pn, ALU.mult))
            n_b = done(V.tensor_scalar(B, pn, -1.0, 1.0, ALU.mult, ALU.add))
            need(n)
            n_a = done(V.tensor_scalar(A, xy_2, y2, 1.0, ALU.add, ALU.add))
            need(n_b)
            n_b = done(V.scalar_tensor_tensor(out=B, in0=pn, scalar=1.0, in1=B, op0=ALU.add, op1=ALU.mult))
            n_d = done(V.scalar_tensor_tensor(out=den, in0=x2, scalar=y2, in1=xy_2, op0=ALU.mult, op1=ALU.add))
            need(n_a)
            done(V.tensor_tensor(Ap, A, pn, ALU.mult))
            need(n_b)
            n = done(V.tensor_tensor(xB, xy_2, B, ALU.mult))
            done(V.tensor_tensor(BB, B, B, ALU.mult))
            need(n_d)
            n_d = done(V.tensor_scalar(den, den, 1.0, MIN_NORM, ALU.add, ALU.max))
            need(n)
            done(V.tensor_tensor(xB, xB, A, ALU.mult))
            n = done(V.tensor_tensor(Ap, Ap, Ap, ALU.mult))
            need(n_d)
            done(V.reciprocal(rden, den))
            need(n)
            n = done(V.tensor_tensor(Ap, Ap, xB, ALU.add))
            done(V.tensor_tensor(alpha, A, gain, ALU.mult))
            need(n)
            done(V.scalar_tensor_tensor(out=num, in0=BB, scalar=y2, in1=Ap, op0=ALU.mult, op1=ALU.add))
            n = done(V.tensor_tensor(over, rden, rden, ALU.mult))
            n_e = done(V.tensor_scalar(beta, B, cb, None, ALU.mult))
            need(n)
            n = done(V.scalar_tensor_tensor(out=num, in0=num, scalar=0.0, in1=over, op0=ALU.max, op1=ALU.mult))
            need(n_e)
            done(V.tensor_tensor(alpha, alpha, rden, ALU.mult))
            done(V.tensor_tensor(beta, beta, rden, ALU.mult))
            done(V.reciprocal(rq, B))
            need(n)
            root(num, inv, root_tmp[:, 0, :], root_tmp[:, 1, :])
            n = done(V.tensor_tensor(zn, num, inv, ALU.mult))
            n_q = done(V.scalar_tensor_tensor(out=rq, in0=rq, scalar=inv_1_y2, in1=den, op0=ALU.mult, op1=ALU.mult))
            need(n)
            done(V.tensor_scalar(w2_, zn, MIN_NORM, BALL, ALU.max, ALU.min))
            n_z = done(V.tensor_scalar(zm, zn, MIN_NORM, None, ALU.max))
            need(n_q)
            n_q = done(V.tensor_scalar(rq, rq, BALL_RQ, None, ALU.min))
            need(n_q)

            def shrink():
                need(n_z)
                return rz, done(V.reciprocal(rz, zm))

            n = artanh_times(w2_, [
                lambda: done(V.scalar_tensor_tensor(out=ratio2, in0=w2_, scalar=1.0, in1=rq, op0=ALU.add, op1=ALU.mult)),
                lambda: done(V.scalar_tensor_tensor(out=ratio2, in0=w2_, scalar=1.0, in1=ratio2, op0=ALU.add, op1=ALU.mult), "ln2_in"),
            ], log2, 3, shrunk, 34, None, shrink)
            need(n)
            done(V.tensor_tensor(alpha, alpha, shrunk, ALU.mult))
            n = done(V.tensor_tensor(beta, beta, shrunk, ALU.mult), "end")
            need(n)

            bias_part = [tmp_a, tmp_b]

            def tangent_of(g):
                rows, n = slice(*GROUPS[g]), GROUPS[g][1] - GROUPS[g][0]
                V.tensor_tensor(bias_part[g % 2][:, 0:n, :], b0_row[:, None, :].broadcast_to([P, n, D]),
                                beta[:, rows, None].broadcast_to([P, n, D]), ALU.mult).then_inc(row_v, 1)
                need(ROW_END + g + 1)
                for t in range(n):
                    j = GROUPS[g][0] + t
                    i = V.scalar_tensor_tensor(out=h_rows[:, j, :], in0=h_rows[:, j, :], scalar=alpha[:, j:j + 1],
                                               in1=bias_part[g % 2][:, t, :], op0=ALU.mult, op1=ALU.add)
                i.then_inc(tangent, 1)

            def tangent_lo(f):
                rows = slice(*FEATS[f])
                dve.wait_ge(feat_hi_ready, f + 1)
                V.tensor_tensor(feat_lo[:, rows, :], h_rows[:, rows, :], feat_hi[:, rows, :].bitcast(F32),
                                ALU.subtract).then_inc(feat_lo_ready, 1)

            ROW_END = n
            assert ROW_END == ROW["end"], ROW_END
            tangent_of(0)
            tangent_of(1)
            for u in range(PLAIN, PAIRS):
                for g in TANGENT_BEFORE.get(u, []):
                    tangent_of(g)
                for f in FEAT_LO_BEFORE.get(u, []):
                    tangent_lo(f)
                split_lo(u, u, u % SLOTS, first=(u < PLAIN + LO_BUFS))

            def post(b, step):
                v0, a0, g0 = (b - 1) * POST_V, (b - 1) * POST_A, (b - 1) * 2
                t0 = (b - 1) * BT
                q = lambda i: ps_[:, i, :]

                def did(ins, count):
                    ins.then_inc(post_v, 1)

                if step == 2:
                    dve.wait_ge(post_g, g0 + 1)
                    did(V.tensor_scalar(q(4), q(2), MIN_NORM, None, ALU.max), 1)
                    did(V.tensor_scalar(q(5), q(2), ATANH_BALL, None, ALU.min), 2)
                    dve.wait_ge(post_v, v0 + 1)
                    did(V.reciprocal(q(6), q(4)), 3)
                    dve.wait_ge(post_v, v0 + 3)
                    did(V.tensor_tensor(q(9), q(5), q(6), ALU.mult), 4)
                    dve.wait_ge(post_v, v0 + 4)
                    did(V.tensor_tensor(q(10), q(9), q(3), ALU.mult), 5)
                    dve.wait_ge(post_v, v0 + 5)
                    did(V.tensor_scalar(q(7), q(10), MIN_NORM, None, ALU.max), POSTV["tanh_in"])
                elif step == 3:
                    dve.wait_ge(post_v, v0 + 6)
                    did(V.reciprocal(q(14), q(7)), 7)
                    dve.wait_ge(post_v, v0 + 7)
                    did(V.tensor_tensor(q(14), q(14), q(9), ALU.mult), 8)
                    dve.wait_ge(post_v, v0 + 8)
                    dve.wait_ge(post_a, a0 + POSTA["tanh"])
                    did(V.scalar_tensor_tensor(out=q(15), in0=q(8), scalar=BALL, in1=q(14), op0=ALU.min, op1=ALU.mult), 9)
                    dve.wait_ge(post_v, v0 + 9)
                    for t in range(BT):
                        i = V.scalar_tensor_tensor(out=x_rows[:, t0 + t, :], in0=tmp_c[:, t, :], scalar=ps_[:, 15, t:t + 1],
                                                   in1=x_rows[:, t0 + t, :], op0=ALU.mult, op1=ALU.add)
                    did(i, POSTV["x"])
                elif step == 4:
                    for t in range(BT):
                        i = V.bn_stats(bn6[:, t, :], x_rows[:, t0 + t, :])
                    did(i, POSTV["bn"])
                elif step == 5:
                    for t in range(BT):
                        i = V.bn_aggr(mv[:, t, :], bn6[:, t, :])
                    did(i, 12)
                    dve.wait_ge(post_v, v0 + 12)
                    did(V.tensor_scalar(q(11), mv[:, 0:BT, 1], LN_EPS, None, ALU.add), POSTV["var"])
                elif step == 6:
                    dve.wait_ge(post_g, g0 + 2)
                    did(V.scalar_tensor_tensor(out=q(13), in0=mv[:, 0:BT, 0], scalar=-1.0, in1=q(12), op0=ALU.mult, op1=ALU.mult),
                        POSTV["shift"])

            def before_post(b, step):
                if step in (4, 5):
                    dve.wait_ge(post_v, (b - 1) * POST_V + POSTV[{4: "x", 5: "bn"}[step]])

            POST_AT = {9: 2, 11: 3, 12: 4, 13: 5, 14: 6}
            with dve.Fori(1, BLOCKS) as b:
                for u in range(PAIRS):
                    before_post(b, POST_AT.get(u))
                    split_lo(b * PAIRS + u, u, u % SLOTS)
                    if u in POST_AT:
                        post(b, POST_AT[u])

            def feat_split(c):
                rows = slice(c * BT, (c + 1) * BT)
                dve.wait_ge(feat_hi_ready, NG + c + 1)
                V.tensor_tensor(feat_lo[:, rows, :], h_rows[:, rows, :], feat_hi[:, rows, :].bitcast(F32),
                                ALU.subtract).then_inc(feat_lo_ready, 1)

            for u in range(PAIRS):
                split_lo(LAYER_UNITS + u, u, u % SLOTS)
                for step in KEPT_POST_DVE.get(u, []):
                    before_post(BLOCKS, step)
                    post(BLOCKS, step)
                for c in KEPT_FEAT_DVE.get(u, []):
                    feat_split(c)

            def last(b, step):
                v0 = (b - 1) * LAST_V
                rows = bass.ds(b * -BT + TILES, BT) if not isinstance(b, int) else slice(TILES - b * BT, TILES - b * BT + BT)
                if step == 0:
                    V.tensor_copy(tmp_c[:, :, :], h_rows[:, rows, :]).then_inc(last_v, 1)
                else:
                    dve.wait_ge(last_p, b)
                    V.tensor_tensor(tmp_c[:, :, :], prod.rearrange("p (t d) -> p t d", d=D),
                                    b1_row[:, None, :].broadcast_to([P, BT, D]), ALU.add).then_inc(last_v, 1)
                    dve.wait_ge(last_v, v0 + 2)
                    V.scalar_tensor_tensor(out=tmp_c[:, :, :].rearrange("p t d -> p (t d)"),
                                           in0=tmp_c[:, :, :].rearrange("p t d -> p (t d)"), scalar=0.0,
                                           in1=x_rows[:, rows, :].rearrange("p t d -> p (t d)"),
                                           op0=ALU.max, op1=ALU.add).then_inc(last_v, 1)

            with dve.Fori(1, BLOCKS) as b:
                for u in range(PAIRS):
                    split_lo(b * PAIRS + (LAYER_UNITS + u), u, u % SLOTS)
                    if u == 0:
                        last(b, 0)
                    if u == 8:
                        last(b, 1)
                dve.wait_ge(stored, b * 16)
            last(BLOCKS, 0)
            last(BLOCKS, 1)


ROW = {"bn0": 1, "bn1": 2, "bn2": 3, "bn3": 4, "aggr": 5, "var": 6, "sums": 7, "ln1_in": 27, "tanh_in": 37,
       "ln2_in": 82, "end": 94}
POSTV = {"tanh_in": 6, "x": 10, "bn": 11, "var": 13, "shift": 14}
POSTA = {"sums": 3, "tanh": 4}
POST_V, POST_A = 14, 5
LASTV = {"h": 1, "y": 3}
LAST_V = 3
GROUPS = [(16, 18), (18, 24), (24, 32), (0, 8), (8, 16)]
FEATS = [(24, 32), (0, 8), (8, 16), (16, 24)]
FEAT_TANGENTS = [3, 4, 5, 2]
NG = len(FEATS)
PRE_SPLIT = 2
TANGENT_BEFORE = {4: [2], 7: [3], 9: [4]}
FEAT_LO_BEFORE = {5: [0], 8: [1], 11: [2], 13: [3]}
FEAT_AT = {8: 0, 9: 1, 11: 2, 13: 3}
KEPT_POST_ACT = {3: [0], 5: [1, 2], 6: [3], 8: [4], 11: [5]}
KEPT_FEAT_ACT = {0: [0], 3: [1], 4: [2], 11: [3]}
KEPT_POST_DVE = {7: [2], 8: [3, 4, 5], 9: [6]}
KEPT_FEAT_DVE = {0: [0], 3: [1], 4: [2], 11: [3]}


def kernel(x, adj, L0_gnn_weight, L0_gnn_bias, L1_gnn_weight, L1_gnn_bias):
    import concourse.bacc as bacc
    from concourse.bass_utils import run_bass_kernel_spmd

    x, adj, w0, w1 = (np.ascontiguousarray(a) for a in (x, adj, L0_gnn_weight, L1_gnn_weight))
    units = adj.reshape(BLOCKS, BLOCK, PAIRS, 2, P).transpose(0, 2, 4, 3, 1)
    units = np.ascontiguousarray(units).reshape(LAYER_UNITS, P, UNIT)
    eye = np.eye(D, dtype=np.float32)
    center = eye - np.float32(1.0 / D)
    consts = np.ascontiguousarray(np.stack([w0.T, w0, w1[:D], w1[D:], eye, center], axis=1))
    arrays = {
        "x": x, "x_t": np.ascontiguousarray(x.T), "adj_units": units, "consts": consts,
        "bias0": np.ascontiguousarray(L0_gnn_bias), "bias1": np.ascontiguousarray(L1_gnn_bias),
    }
    nc = bacc.Bacc("TRN2", target_bir_lowering=False, num_devices=1, dynamic_dma_scratch_size=1024)
    args = [nc.dram_tensor(k, a.shape, mybir.dt.from_np(a.dtype), kind="ExternalInput").ap() for k, a in arrays.items()]
    args.append(nc.dram_tensor("out", (N, D), F32, kind="ExternalOutput").ap())
    two_layers(nc, *args)
    got = run_bass_kernel_spmd(nc, [arrays], core_ids=[0])
    return got.results[0]["out"]
```

```python
from contextlib import ExitStack

import numpy as np

import concourse.bass as bass
from concourse import mybir

F32 = mybir.dt.float32
F32R = mybir.dt.float32r
I32 = mybir.dt.int32
ACT = mybir.ActivationFunctionType
ALU = mybir.AluOpType
AX_X = mybir.AxisListType.X

P = 128
N = 4096
D = 128
TILES = N // P
BLOCK = 1024
BLOCKS = N // BLOCK
BT = BLOCK // P
PAIRS = TILES // 2
BANK = 512
HALVES = BLOCK // BANK
HALF = BT // 2
UNIT = 2 * BLOCK
SLOTS = 8
HI_BUFS, LO_BUFS = 4, 4
LAYER_UNITS = BLOCKS * PAIRS
PLAIN = 4
assert PLAIN == HI_BUFS == LO_BUFS
KEPT = 8

LN_EPS = 1e-5
MIN_NORM = 1e-15
BALL = float(np.float32(1.0 - 1e-5))
ATANH_CLIP = float(np.float32(1.0 - 1e-7))
ATANH_BALL = float(0.5 * (np.log1p(np.float64(np.float32(BALL))) - np.log1p(-np.float64(np.float32(BALL)))))
BALL_RQ = float(1.0 / ((1.0 - np.float64(np.float32(BALL))) * (1.0 + np.float64(np.float32(BALL)))))
SERIES_BELOW = 0.15
SERIES = [1.0 / (2 * k + 1) for k in range(1, 4)]

SPLIT_KEPT = HI_BUFS
ORDER0 = list(range(PAIRS // 2, PAIRS)) + list(range(PAIRS // 2))
ORDER1 = ORDER0[PAIRS - SPLIT_KEPT:] + ORDER0[PAIRS - KEPT:PAIRS - SPLIT_KEPT] + list(range(PAIRS // 2, PAIRS))

W0T, W0, W1_SELF, W1_AGG, EYE, CENTER, CONSTS = range(7)
assert CENTER == CONSTS - 1


def two_layers(nc, x, x_t, adj_units, consts, bias0, bias1, out):
    with ExitStack() as ctx:
        def sb(name, shape, dt=F32):
            return ctx.enter_context(nc.sbuf_tensor(name, shape, dt))

        def sem(name):
            return ctx.enter_context(nc.semaphore(name))

        ring = sb("ring", [P, SLOTS, UNIT])
        adj_hi = sb("adj_hi", [P, HI_BUFS, UNIT], F32R)
        adj_lo = sb("adj_lo", [P, LO_BUFS, UNIT], F32R)
        x_rows = sb("x_rows", [P, TILES, D])
        h_rows = sb("h_rows", [P, TILES, D])
        feat_hi = sb("feat_hi", [P, TILES, D], F32R)
        feat_lo = sb("feat_lo", [P, TILES, D], F32R)
        tmp_a = sb("tmp_a", [P, BT, D])
        tmp_b = sb("tmp_b", [P, BT, D])
        tmp_c = sb("tmp_c", [P, BT, D])
        cst = sb("cst", [P, CONSTS, D])
        b0_col = sb("b0_col", [P, 1])
        b0_row = sb("b0_row", [P, D])
        b1_row = sb("b1_row", [P, D])
        ones = sb("ones", [P, P])
        b0_sq = sb("b0_sq", [P, 1])
        w0t_v = sb("w0t_v", [P, D + 1])
        bias_sc = sb("bias_sc", [P, 12])
        bn6 = sb("bn6", [P, TILES, 6])
        mv = sb("mv", [P, TILES, 2])
        sc = sb("sc", [P, 40, TILES])
        row_sums = sb("row_sums", [P, TILES, 2])
        root_tmp = sb("root_tmp", [P, 6, TILES])
        post_sc = sb("post_sc", [P, 16, BT])
        half_b = sb("half_b", [P, 2, BT])
        mhalf_b = sb("mhalf_b", [P, BT])

        psum = ctx.enter_context(nc.psum_tensor("psum", [P, 8, BANK], F32))
        turned = psum[:, 4:6, :].rearrange("p a b -> p (a b)")
        prod = psum[:, 6:8, :].rearrange("p a b -> p (a b)")

        center_loaded = sem("center_loaded")
        const_loaded = sem("const_loaded")
        xt_loaded = [sem(f"xt_loaded{c}") for c in range(BLOCKS)]
        x_loaded = [sem(f"x_loaded{c}") for c in range(BLOCKS)]
        slot_loaded = [sem(f"slot_loaded{s}") for s in range(SLOTS)]
        made = sem("made")
        setup_v = sem("setup_v")
        setup_p = sem("setup_p")
        setup_g = sem("setup_g")
        setup_a = sem("setup_a")
        centered = sem("centered")
        relued = sem("relued")
        squared = sem("squared")
        projected = sem("projected")
        kept = sem("kept")
        reduced = sem("reduced")
        row_v = sem("row_v")
        row_a = sem("row_a")
        tangent = sem("tangent")
        feat_hi_ready = sem("feat_hi_ready")
        feat_lo_ready = sem("feat_lo_ready")
        hi_ready = sem("hi_ready")
        lo_ready = sem("lo_ready")
        unit_done = sem("unit_done")
        acc_read = sem("acc_read")
        turn_done = sem("turn_done")
        post_a = sem("post_a")
        post_v = sem("post_v")
        post_g = sem("post_g")
        last_v = sem("last_v")
        last_a = sem("last_a")
        last_p = sem("last_p")
        half_done = sem("half_done")
        stored = sem("stored")

        ident = cst[:, EYE, :]

        (b_sumsq, b_norm_raw, b_norm, b_tanh, y_norm, inv_b_norm, y2, cb, cb_2, y2_rest, inv_1_y2, table_load) = (
            bias_sc[:, i:i + 1] for i in range(12))

        rstd = sc[:, 3, :]
        (w1, ratio1, log1, stretched, tanh_arg, tanh_out, unit, xy_p, pn, x2, xy_2, gain, A, B, den, Ap, xB, BB,
         rden, rq) = (sc[:, 14 + i, :] for i in range(20))
        alpha, beta, num, over, inv = w1, log1, stretched, tanh_arg, xB
        zn, w2_, zm, rz, ratio2, log2, shrunk = tanh_out, unit, xy_p, pn, x2, xy_2, gain

        s_norm, relu_norm = post_sc[:, 2, :], post_sc[:, 3, :]
        (s_kept, s_ball, inv_s, tanh_in, relu_tanh, shrink_s, relu_t, post_var, post_rstd, post_shift, inv_relu,
         relu_gain) = (post_sc[:, 4 + i, :] for i in range(12))

        def slot_of(u, layer):
            return (u - (SPLIT_KEPT if layer else 0)) % SLOTS

        def fill_of(u, layer):
            return u // SLOTS + (LAYER_UNITS // SLOTS if layer else 1)

        def splits(u, layer):
            return u + 1 - PLAIN + (LAYER_UNITS - SPLIT_KEPT if layer else 0)

        xt_sb = ring[:, 6:8, :].rearrange("p a b -> p (a b)")
        ut = [ring[:, 5, i * BLOCK:(i + 1) * BLOCK] for i in range(2)]
        ut_sq = [ring[:, 4, i * BLOCK:(i + 1) * BLOCK] for i in range(2)]
        mx_sq = [buf[:, i * HALF:(i + 1) * HALF, :] for buf in (tmp_a, tmp_b) for i in range(2)]
        MX_SQ_BUFS = len(mx_sq)
        cen = [psum[:, 2 * i:2 * i + 2, :].rearrange("p a b -> p (a b)") for i in range(2)]
        mx_all = psum[:, 4:8, :].rearrange("p a (i c) -> p (a i) c", c=2 * D)
        setup_ps = psum[:, 7, 0:2]

        block = ctx.enter_context(nc.Block())

        @block.sync
        def _(sp):
            x_tiles = x.rearrange("(t p) d -> p t d", p=P)
            sp.dma_start(cst[:, CENTER, :], consts[:, CENTER, :]).then_inc(center_loaded, 16)
            sp.dma_start(xt_sb[:, 0:BLOCK], x_t[:, 0:BLOCK]).then_inc(xt_loaded[0], 16)
            sp.dma_start(cst[:, 0:CENTER, :], consts[:, 0:CENTER, :]).then_inc(const_loaded, 16)
            sp.dma_start(b0_col[:, :], bias0.rearrange("(d a) -> d a", a=1)).then_inc(const_loaded, 16)
            sp.dma_start(b0_row[:, :], bias0.rearrange("(a d) -> a d", a=1).broadcast_to([P, D])).then_inc(const_loaded, 16)
            sp.dma_start(b1_row[:, :], bias1.rearrange("(a d) -> a d", a=1).broadcast_to([P, D])).then_inc(const_loaded, 16)
            for c in range(BLOCKS):
                if c > 0:
                    sp.dma_start(xt_sb[:, c * BLOCK:(c + 1) * BLOCK], x_t[:, c * BLOCK:(c + 1) * BLOCK]).then_inc(xt_loaded[c], 16)
                sp.dma_start(x_rows[:, c * BT:(c + 1) * BT, :], x_tiles[:, c * BT:(c + 1) * BT, :]).then_inc(x_loaded[c], 16)

            def load(u, layer, unit):
                slot = slot_of(u, layer)
                sp.dma_start(ring[:, slot, :], adj_units[unit]).then_inc(slot_loaded[slot], 16)

            for u in range(PLAIN):
                load(u, 0, ORDER0[u])
            sp.wait_ge(projected, 2 * BLOCKS)
            for u in range(PLAIN, SLOTS):
                load(u, 0, ORDER0[u])
            for u in range(SLOTS, PAIRS):
                if u - SLOTS < PLAIN:
                    sp.wait_ge(unit_done, u - SLOTS + 1)
                else:
                    sp.wait_ge(lo_ready, splits(u - SLOTS, 0))
                load(u, 0, ORDER0[u])
            with sp.Fori(1, BLOCKS) as b:
                for u in range(PAIRS):
                    sp.wait_ge(lo_ready, b * PAIRS + splits(u - SLOTS, 0))
                    load(u, 0, b * PAIRS + ORDER0[u])
            for u in range(KEPT, PAIRS):
                sp.wait_ge(lo_ready, splits(u - SLOTS, 1))
                load(u, 1, (BLOCKS - 1) * PAIRS + ORDER1[u])
            with sp.Fori(1, BLOCKS) as b:
                for u in range(PAIRS):
                    sp.wait_ge(lo_ready, b * PAIRS + splits(u - SLOTS, 1))
                    load(u, 1, b * (-PAIRS) + ((BLOCKS - 1) * PAIRS + ORDER1[u]))

        @block.gpsimd
        def _(pool):
            nc.gpsimd.memset(ones[:, :], 1.0).then_inc(made, 1)
            nc.gpsimd.memset(half_b[:, :, :], 0.5).then_inc(made, 1)
            nc.gpsimd.memset(mhalf_b[:, :], -0.5).then_inc(made, 1)
            pool.wait_ge(made, 3)
            pool.wait_ge(setup_v, 3)
            nc.gpsimd.tensor_tensor(b_norm_raw, b_sumsq, half_b[:, 0, 0:1], ALU.pow).then_inc(setup_g, 1)
            with pool.Fori(1, BLOCKS + 1) as b:
                pool.wait_ge(post_a, (b - 1) * POST_A + POSTA["sums"])
                nc.gpsimd.tensor_tensor(post_sc[:, 2:4, :], post_sc[:, 0:2, :], half_b[:, :, :], ALU.pow).then_inc(post_g, 1)
                pool.wait_ge(post_v, (b - 1) * POST_V + POSTV["var"])
                nc.gpsimd.tensor_tensor(post_rstd, post_var, mhalf_b[:, :], ALU.pow).then_inc(post_g, 1)

        @block.tensor
        def _(pe):
            def warm_up(count):
                for _ in range(count):
                    nc.tensor.matmul(turned[:, 0:P], ones[:, :], ones[:, :], start=True, stop=True)

            def center(c):
                pe.wait_ge(xt_loaded[c], 16)
                if c >= 2:
                    pe.wait_ge(relued, c - 1)
                for h in range(HALVES):
                    q = slice(h * BANK, (h + 1) * BANK)
                    mm = nc.tensor.matmul(cen[c % 2][:, q], cst[:, CENTER, :], xt_sb[:, c * BLOCK + h * BANK:c * BLOCK + (h + 1) * BANK],
                                          start=True, stop=True)
                mm.then_inc(centered, 1)

            def project(m):
                c, first = m // 2, m % 2 * HALF
                if m == 0:
                    pe.wait_ge(setup_v, 3)
                if m % 2 == 0:
                    pe.wait_ge(relued, c + 1)
                if m >= 2:
                    pe.wait_ge(kept, 3 * (m - 2) + 2)
                for t in range(first, first + HALF):
                    nc.tensor.matmul(mx_all[:, t, 0:D + 1], ut[c % 2][:, t * P:(t + 1) * P], w0t_v[:, :], start=True, stop=True)
                if m % 2 == 0:
                    pe.wait_ge(squared, c + 1)
                for t in range(first, first + HALF):
                    mm = nc.tensor.matmul(mx_all[:, t, D + 1:D + 2], ut_sq[c % 2][:, t * P:(t + 1) * P], ones[:, 0:1], start=True, stop=True)
                mm.then_inc(projected, 1)

            pe.wait_ge(made, 3)
            warm_up(9)
            pe.wait_ge(center_loaded, 16)
            center(0)
            pe.wait_ge(const_loaded, 64)
            pe.wait_ge(setup_v, 1)
            nc.tensor.matmul(setup_ps[:, 0:1], cst[:, W0, :], b0_col[:, :], start=True, stop=True)
            nc.tensor.matmul(setup_ps[:, 1:2], ones[:, :], b0_sq[:, :], start=True, stop=True).then_inc(setup_p, 1)
            pe.wait_ge(setup_v, 3)

            for c in range(BLOCKS):
                if c + 1 < BLOCKS:
                    center(c + 1)
                project(2 * c)
                project(2 * c + 1)

            def multiply(layer, b, feat_waits, hooks, plain=0, halves_apart=False):
                acc0 = (b % 2) * HALVES
                for u, k in enumerate(ORDER1 if layer else ORDER0):
                    if u in hooks:
                        hooks[u]()
                    if u < plain and 2 * k in [first for first, _ in GROUPS]:
                        pe.wait_ge(tangent, [first for first, _ in GROUPS].index(2 * k) + 1)
                    if k in feat_waits:
                        pe.wait_ge(feat_hi_ready, feat_waits[k])
                        pe.wait_ge(feat_lo_ready, feat_waits[k])
                    if u < plain:
                        pe.wait_ge(slot_loaded[u], 16)
                        for e in range(2):
                            for h in range(HALVES):
                                mm = nc.tensor.matmul(psum[:, acc0 + h, :], h_rows[:, 2 * k + e, :],
                                                      ring[:, u, e * BLOCK + h * BANK:e * BLOCK + (h + 1) * BANK],
                                                      start=(u == 0 and e == 0), stop=False)
                        mm.then_inc(unit_done, 1)
                        continue
                    hb, lb = u % HI_BUFS, u % LO_BUFS
                    if halves_apart and u == PAIRS - 1:
                        pe.wait_ge(hi_ready, b * PAIRS + splits(u, layer))
                        pe.wait_ge(lo_ready, b * PAIRS + splits(u, layer))
                        for h in range(HALVES):
                            for w, buf in ((feat_hi, adj_hi), (feat_lo, adj_hi), (feat_hi, adj_lo)):
                                for e in range(2):
                                    mm = nc.tensor.matmul(psum[:, acc0 + h, :], w[:, 2 * k + e, :],
                                                          buf[:, hb, e * BLOCK + h * BANK:e * BLOCK + (h + 1) * BANK],
                                                          start=False, stop=(e == 1 and buf is adj_lo))
                            mm.then_inc(half_done, 1)
                        continue
                    for part, ready, buf in (("hi", hi_ready, adj_hi[:, hb, :]), ("lo", lo_ready, adj_lo[:, lb, :])):
                        pe.wait_ge(ready, b * PAIRS + splits(u, layer))
                        for e in range(2):
                            for w in ((feat_hi, feat_lo) if part == "hi" else (feat_hi,)):
                                for h in range(HALVES):
                                    mm = nc.tensor.matmul(psum[:, acc0 + h, :], w[:, 2 * k + e, :],
                                                          buf[:, e * BLOCK + h * BANK:e * BLOCK + (h + 1) * BANK],
                                                          start=(plain == 0 and u == 0 and part == "hi" and e == 0 and w is feat_hi),
                                                          stop=(u == PAIRS - 1 and part == "lo" and e == 1))
                    mm.then_inc(unit_done, 1)

            def turn(src, waits):
                for s, v in waits:
                    pe.wait_ge(s, v)
                for t in range(BT):
                    mm = nc.tensor.transpose(turned[:, t * P:(t + 1) * P], src[:, t, :], ident)
                mm.then_inc(turn_done, 1)

            pe.wait_ge(row_v, ROW["ln2_in"])
            warm_up(5)
            pe.wait_ge(kept, 3 * 2 * BLOCKS - 1)
            multiply(0, 0, {first // 2: g + 1 for g, (first, _) in enumerate(FEATS[:-1])}, {}, plain=PLAIN)
            pe.wait_ge(feat_hi_ready, len(FEATS))
            pe.wait_ge(feat_lo_ready, len(FEATS))
            with pe.Fori(1, BLOCKS) as b:
                multiply(0, b, {}, {
                    1: lambda: turn(tmp_a, [(acc_read, b)])})
            multiply(1, 0, {first // 2: len(FEATS) + f + 1 for f, (first, _) in enumerate(FEATS1)}, {
                1: lambda: turn(tmp_a, [(acc_read, BLOCKS)])})

            def last_products(n, tiles=range(BT)):
                pe.wait_ge(last_a, n)
                for t in tiles:
                    nc.tensor.matmul(prod[:, t * D:(t + 1) * D], tmp_b[:, t, :], cst[:, W1_SELF, :], start=True, stop=False)
                    mm = nc.tensor.matmul(prod[:, t * D:(t + 1) * D], tmp_a[:, t, :], cst[:, W1_AGG, :], start=False, stop=True)
                mm.then_inc(last_p, 1)

            def turn_h(b):
                turn(tmp_c, [(last_v, (b - 1) * LAST_V + LASTV["h"])])

            with pe.Fori(1, BLOCKS - 1) as b:
                multiply(1, b, {}, {1: lambda: turn_h(b), 3: lambda: last_products(2 * b)})
            b = BLOCKS - 1
            multiply(1, b, {}, {
                1: lambda: turn_h(b), 3: lambda: last_products(2 * b), PAIRS - 1: lambda: turn_h(BLOCKS)}, halves_apart=True)
            for h in range(HALVES):
                last_products(2 * b + 1 + (h + 1), range(h * HALF, (h + 1) * HALF))

        @block.scalar
        def _(act):
            def split_hi(layer, b, u, first=False):
                n = b * PAIRS + (layer * LAYER_UNITS + u)
                act.wait_ge(slot_loaded[slot_of(u, layer)], (b * (PAIRS // SLOTS) + fill_of(u, layer)) * 16)
                if not first:
                    act.wait_ge(unit_done, n - HI_BUFS + 1)
                nc.scalar.activation(adj_hi[:, u % HI_BUFS, :], ring[:, slot_of(u, layer), :], ACT.Copy).then_inc(hi_ready, 1)

            for c in range(BLOCKS + 1):
                if c < BLOCKS:
                    act.wait_ge(centered, c + 1)
                    if c >= 2:
                        act.wait_ge(projected, 2 * (c - 1))
                    nc.scalar.activation(ut[c % 2], cen[c % 2], ACT.Relu).then_inc(relued, 1)
                if c == 1:
                    act.wait_ge(setup_v, 4)
                    nc.scalar.activation(b_tanh, b_norm, ACT.Tanh).then_inc(setup_a, 1)
                if c:
                    for m in (2 * c - 2, 2 * c - 1):
                        here, tiles = slice(m % 2 * HALF, (m % 2 + 1) * HALF), slice(m * HALF, (m + 1) * HALF)
                        act.wait_ge(projected, m + 1)
                        nc.scalar.activation(h_rows[:, tiles, :], mx_all[:, here, 0:D], ACT.Copy).then_inc(kept, 1)
                        nc.scalar.activation(row_sums[:, tiles, :], mx_all[:, here, D:D + 2], ACT.Copy).then_inc(kept, 1)
                        act.wait_ge(kept, 3 * m + 1)
                        if m >= MX_SQ_BUFS:
                            act.wait_ge(reduced, m - MX_SQ_BUFS + 1)
                        nc.scalar.activation(mx_sq[m % MX_SQ_BUFS], h_rows[:, tiles, :], ACT.Square).then_inc(kept, 1)
            act.wait_ge(row_v, ROW["ln1_in"])
            nc.scalar.activation(log1, ratio1, ACT.Ln).then_inc(row_a, 1)
            act.wait_ge(row_v, ROW["tanh_in"])
            nc.scalar.activation(tanh_out, tanh_arg, ACT.Tanh).then_inc(row_a, 1)
            for u in range(PLAIN, PLAIN + PRE_SPLIT):
                split_hi(0, 0, u, first=True)
            act.wait_ge(row_v, ROW["ln2_in"])
            nc.scalar.activation(log2, ratio2, ACT.Ln).then_inc(row_a, 1)

            def copy_acc(count_before, dst, b):
                act.wait_ge(unit_done, count_before)
                acc = psum[:, bass.ds(((b + 1) % 2) * HALVES, HALVES), :]
                return nc.scalar.activation(dst[:, :, :].rearrange("p t d -> p (t d)"), acc.rearrange("p a b -> p (a b)"), ACT.Copy)

            for u in range(PLAIN + PRE_SPLIT, PAIRS + 1):
                if u in FEAT_AT:
                    f = FEAT_AT[u]
                    rows = slice(*FEATS[f])
                    act.wait_ge(tangent, FEAT_TANGENTS[f])
                    nc.scalar.activation(feat_hi[:, rows, :], h_rows[:, rows, :], ACT.Copy).then_inc(feat_hi_ready, 1)
                if u < PAIRS:
                    split_hi(0, 0, u, first=(u < PLAIN + HI_BUFS))
            nc.scalar.activation(table_load, b_norm, ACT.Tanh).then_inc(setup_a, 1)

            def post(b, step):
                base = (b - 1) * POST_A
                if step == 0:
                    i = copy_acc(b * PAIRS, tmp_a, b)
                    i.then_inc(acc_read, 1)
                elif step == 1:
                    act.wait_ge(turn_done, b)
                    for t in range(BT):
                        i = nc.scalar.activation(tmp_b[:, t, :], turned[:, t * D:(t + 1) * D], ACT.Square, accum_out=post_sc[:, 0, t:t + 1])
                    i.then_inc(post_a, 1)
                elif step == 2:
                    nc.scalar.activation(tmp_c[:, :, :].rearrange("p t d -> p (t d)"), turned, ACT.Relu).then_inc(post_a, 1)
                elif step == 3:
                    act.wait_ge(post_a, base + 2)
                    for t in range(BT):
                        i = nc.scalar.activation(tmp_b[:, t, :], tmp_c[:, t, :], ACT.Square, accum_out=post_sc[:, 1, t:t + 1])
                    i.then_inc(post_a, 1)
                elif step == 4:
                    act.wait_ge(post_v, (b - 1) * POST_V + POSTV["tanh_in"])
                    nc.scalar.activation(relu_tanh, tanh_in, ACT.Tanh).then_inc(post_a, 1)
                elif step == 5:
                    act.wait_ge(post_v, (b - 1) * POST_V + POSTV["shift"])
                    for t in range(BT):
                        tile = (b - 1) * BT + t
                        i = nc.scalar.activation(h_rows[:, tile, :], x_rows[:, tile, :], ACT.Relu,
                                                 bias=post_shift[:, t:t + 1], scale=post_rstd[:, t:t + 1])
                    i.then_inc(post_a, 1)

            POST_AT = {3: 0, 5: 1, 6: 2, 7: 3, 9: 4}

            def layer0_block(b, finish_before):
                for u in range(PAIRS):
                    if u == 1 and finish_before:
                        post(b - 1, 5)
                    if u in POST_AT:
                        post(b, POST_AT[u])
                    split_hi(0, b, u)

            layer0_block(1, False)
            with act.Fori(2, BLOCKS) as b:
                layer0_block(b, True)

            def feat_split(f):
                first, end = FEATS1[f]
                act.wait_ge(post_a, ((end - 1) // BT + 1) * POST_A)
                act.wait_ge(unit_done, LAYER_UNITS - PAIRS + ORDER0.index((end - 1) // 2) + 1)
                nc.scalar.activation(feat_hi[:, first:end, :], h_rows[:, first:end, :], ACT.Copy).then_inc(feat_hi_ready, 1)

            for u in range(PAIRS):
                if u == KEPT_H_AT:
                    post(BLOCKS - 1, 5)
                for step in KEPT_POST_ACT.get(u, []):
                    post(BLOCKS, step)
                for f in KEPT_FEAT_ACT.get(u, []):
                    feat_split(f)
                if u >= SPLIT_KEPT:
                    split_hi(1, 0, u)

            def last(b, step):
                if step == 0:
                    copy_acc(b * PAIRS + LAYER_UNITS, tmp_a, b).then_inc(last_a, 1)
                elif step == 1:
                    act.wait_ge(turn_done, b + BLOCKS)
                    nc.scalar.activation(tmp_b[:, :, :].rearrange("p t d -> p (t d)"), turned, ACT.Copy).then_inc(last_a, 1)
                else:
                    act.wait_ge(last_v, (b - 1) * LAST_V + LASTV["y"])
                    act.dma_start(out_blocks[b * -1 + BLOCKS], tmp_c[:, :, :]).then_inc(stored, 16)

            out_blocks = out.rearrange("(g t p) d -> g p t d", p=P, t=BT)
            LAST_AT = {2: 0, 5: 1, 14: 2}

            def layer1_block(b):
                for u in range(PAIRS):
                    if u in LAST_AT:
                        last(b, LAST_AT[u])
                    split_hi(1, b, u)

            with act.Fori(1, BLOCKS - 1) as b:
                layer1_block(b)
            layer1_block(BLOCKS - 1)
            last(BLOCKS, 1)
            for h in range(HALVES):
                tiles = slice(h * HALF, (h + 1) * HALF)
                act.wait_ge(half_done, h + 1)
                nc.scalar.activation(tmp_a[:, tiles, :].rearrange("p t d -> p (t d)"),
                                     psum[:, (BLOCKS - 1) % 2 * HALVES + h, :], ACT.Copy).then_inc(last_a, 1)
            for h in range(HALVES):
                tiles = slice(h * HALF, (h + 1) * HALF)
                act.wait_ge(last_v, (BLOCKS - 1) * LAST_V + LASTV["h"] + 2 * (h + 1))
                act.dma_start(out_blocks[0][:, tiles, :], tmp_c[:, tiles, :]).then_inc(stored, 16)
            act.wait_ge(stored, 16 * (BLOCKS - 1 + HALVES))

        @block.vector
        def _(dve):
            V = nc.vector

            def steps(s, names):
                state = {"n": 0}

                def done(ins, name=None):
                    ins.then_inc(s, 1)
                    state["n"] += 1
                    if name:
                        assert names[name] == state["n"], (name, state["n"])
                    return state["n"]
                return done

            def split_lo(layer, b, u, first=False):
                n = b * PAIRS + (layer * LAYER_UNITS + u)
                dve.wait_ge(hi_ready, b * PAIRS + splits(u, layer))
                if not first:
                    dve.wait_ge(unit_done, n - LO_BUFS + 1)
                V.tensor_tensor(adj_lo[:, u % LO_BUFS, :], ring[:, slot_of(u, layer), :], adj_hi[:, u % HI_BUFS, :].bitcast(F32),
                                ALU.subtract).then_inc(lo_ready, 1)

            done = steps(row_v, ROW)
            dot_b = row_sums[:, :, 0]
            dve.wait_ge(const_loaded, 64)
            V.tensor_tensor(b0_sq[:, :], b0_col[:, :], b0_col[:, :], ALU.mult).then_inc(setup_v, 1)
            dve.wait_ge(setup_p, 1)
            V.tensor_copy(w0t_v[:, D:D + 1], setup_ps[:, 0:1])
            V.tensor_copy(w0t_v[:, 0:D], cst[:, W0T, :]).then_inc(setup_v, 1)
            V.tensor_copy(b_sumsq, setup_ps[:, 1:2]).then_inc(setup_v, 1)

            def square_ut(c):
                dve.wait_ge(relued, c + 1)
                if c >= 2:
                    dve.wait_ge(projected, 2 * (c - 1))
                V.tensor_tensor(ut_sq[c % 2], ut[c % 2], ut[c % 2], ALU.mult).then_inc(squared, 1)

            def statistics(c):
                dve.wait_ge(x_loaded[c], 16)
                for t in range(c * BT, (c + 1) * BT):
                    i = V.bn_stats(bn6[:, t, :], x_rows[:, t, :])
                done(i, f"bn{c}")

            square_ut(0)
            statistics(0)
            square_ut(1)
            dve.wait_ge(setup_g, 1)
            V.tensor_scalar(b_norm, b_norm_raw, MIN_NORM, None, ALU.max).then_inc(setup_v, 1)
            dve.wait_ge(setup_a, 1)
            V.tensor_scalar(y_norm, b_tanh, BALL, None, ALU.min).then_inc(setup_v, 1)
            dve.wait_ge(setup_v, 5)
            V.reciprocal(inv_b_norm, b_norm).then_inc(setup_v, 1)
            V.tensor_tensor(y2, y_norm, y_norm, ALU.mult).then_inc(setup_v, 1)
            dve.wait_ge(setup_v, 6)
            V.tensor_tensor(cb, y_norm, inv_b_norm, ALU.mult).then_inc(setup_v, 1)
            dve.wait_ge(setup_v, 8)
            V.tensor_scalar(cb_2, cb, 2.0, None, ALU.mult).then_inc(setup_v, 1)
            V.tensor_scalar(y2_rest, y2, -1.0, 1.0, ALU.mult, ALU.add).then_inc(setup_v, 1)
            dve.wait_ge(setup_v, 10)
            V.reciprocal(inv_1_y2, y2_rest).then_inc(setup_v, 1)
            dve.wait_ge(setup_v, 11)

            def aggregate(c):
                dve.wait_ge(row_v, ROW[f"bn{c}"])
                for t in range(c * BT, (c + 1) * BT):
                    i = V.bn_aggr(mv[:, t, :], bn6[:, t, :])
                if c == BLOCKS - 1:
                    done(i, "aggr")
                    dve.wait_ge(row_v, ROW["aggr"])
                    done(V.tensor_scalar(sc[:, 0, :], mv[:, :, 1], LN_EPS, None, ALU.add), "var")

            for c in range(BLOCKS):
                if c + 1 < BLOCKS:
                    statistics(c + 1)
                if c == BLOCKS - 1:
                    aggregate(c)
                for m in (2 * c, 2 * c + 1):
                    dve.wait_ge(kept, 3 * m + 3)
                    V.tensor_reduce(sc[:, 2, m * HALF:(m + 1) * HALF], mx_sq[m % MX_SQ_BUFS], AX_X, ALU.add).then_inc(reduced, 1)
                if c + 2 < BLOCKS:
                    square_ut(c + 2)
                if c < BLOCKS - 1:
                    aggregate(c)
            dve.wait_ge(reduced, 2 * BLOCKS)
            dve.wait_ge(kept, 3 * 2 * BLOCKS)
            done(V.tensor_copy(sc[:, 1, :], row_sums[:, :, 1]), "sums")

            def need(n):
                dve.wait_ge(row_v, n)

            def artanh_times(w, ratio_steps, log, logs, out, tmp, out_name, factor):
                s, w2, wk, wm, hk = (sc[:, tmp + i, :] for i in range(5))
                i_r = ratio_steps[0]()
                i_w2 = done(V.tensor_tensor(w2, w, w, ALU.mult))
                i_hk = done(V.tensor_scalar(hk, w, SERIES_BELOW, 0.5, ALU.is_ge, ALU.mult))
                need(i_r)
                i_r = ratio_steps[1]()
                need(i_w2)
                i_s = done(V.tensor_scalar(s, w2, SERIES[2], None, ALU.mult))
                for step in ratio_steps[2:]:
                    need(i_r)
                    i_r = step()
                k, i_k = factor()
                need(i_s)
                i_s = done(V.scalar_tensor_tensor(out=s, in0=s, scalar=SERIES[1], in1=w2, op0=ALU.add, op1=ALU.mult))
                need(i_k)
                i_wk = done(V.tensor_tensor(wk, w, k, ALU.mult))
                need(i_s)
                i_s = done(V.scalar_tensor_tensor(out=s, in0=s, scalar=SERIES[0], in1=w2, op0=ALU.add, op1=ALU.mult))
                need(max(i_wk, i_hk))
                i_wm = done(V.scalar_tensor_tensor(out=wm, in0=w, scalar=SERIES_BELOW, in1=wk, op0=ALU.is_lt, op1=ALU.mult))
                i_hk = done(V.tensor_tensor(hk, hk, k, ALU.mult))
                need(i_wm)
                i_s = done(V.scalar_tensor_tensor(out=s, in0=s, scalar=1.0, in1=wm, op0=ALU.add, op1=ALU.mult))
                need(i_hk)
                dve.wait_ge(row_a, logs)
                i_l = done(V.tensor_tensor(hk, log, hk, ALU.mult))
                need(i_l)
                return done(V.tensor_tensor(out, hk, s, ALU.add), out_name)

            def root(v, y, a, b):
                i = done(V.tensor_scalar(a.bitcast(I32), v.bitcast(I32), 1, None, ALU.logical_shift_right))
                need(i)
                i = done(V.tensor_scalar(y.bitcast(I32), a.bitcast(I32), -1, 0x5F3759DF, ALU.mult, ALU.add))
                need(i)
                i = done(V.tensor_tensor(a, y, v, ALU.mult))
                need(i)
                i = done(V.tensor_tensor(a, a, y, ALU.mult))
                need(i)
                i = done(V.tensor_scalar(b, a, 0.3755269, -1.2521496, ALU.mult, ALU.add))
                need(i)
                i = done(V.tensor_tensor(b, b, a, ALU.mult))
                need(i)
                i = done(V.scalar_tensor_tensor(out=y, in0=b, scalar=1.8766229, in1=y, op0=ALU.add, op1=ALU.mult))
                need(i)
                i = done(V.scalar_tensor_tensor(out=a, in0=y, scalar=-0.5, in1=v, op0=ALU.mult, op1=ALU.mult))
                need(i)
                i = done(V.tensor_tensor(a, a, y, ALU.mult))
                need(i)
                i = done(V.scalar_tensor_tensor(out=y, in0=a, scalar=1.5, in1=y, op0=ALU.add, op1=ALU.mult))
                need(i)

            need(ROW["sums"])
            root(sc[:, 0:3, :], sc[:, 3:6, :], root_tmp[:, 0:3, :], root_tmp[:, 3:6, :])
            n = done(V.tensor_tensor(sc[:, 6:8, :], sc[:, 4:6, :], sc[:, 1:3, :], ALU.mult))
            need(n)
            n = done(V.tensor_tensor(sc[:, 8:10, :], sc[:, 6:8, :], rstd[:, None, :].broadcast_to([P, 2, TILES]), ALU.mult))
            need(n)
            n = done(V.tensor_scalar(w1, sc[:, 8, :], MIN_NORM, ATANH_CLIP, ALU.max, ALU.min))
            norms = done(V.tensor_scalar(sc[:, 10:12, :], sc[:, 8:10, :], MIN_NORM, None, ALU.max))
            need(n)

            def stretch():
                need(norms)
                n = done(V.reciprocal(sc[:, 12:14, :], sc[:, 10:12, :]))
                need(n)
                return stretched, done(V.tensor_tensor(stretched, sc[:, 11, :], sc[:, 12, :], ALU.mult))

            artanh_times(w1, [
                lambda: done(V.tensor_scalar(ratio1, w1, -1.0, 1.0, ALU.mult, ALU.add)),
                lambda: done(V.reciprocal(ratio1, ratio1)),
                lambda: done(V.scalar_tensor_tensor(out=ratio1, in0=w1, scalar=1.0, in1=ratio1, op0=ALU.add, op1=ALU.mult), "ln1_in"),
            ], log1, 1, tanh_arg, 34, "tanh_in", stretch)
            n = done(V.tensor_tensor(unit, rstd, sc[:, 13, :], ALU.mult))
            need(n)
            done(V.scalar_tensor_tensor(out=xy_p, in0=unit, scalar=cb_2, in1=dot_b, op0=ALU.mult, op1=ALU.mult))
            dve.wait_ge(row_a, 2)
            n = done(V.tensor_scalar(pn, tanh_out, BALL, None, ALU.min))
            need(n)
            done(V.tensor_tensor(x2, pn, pn, ALU.mult))
            n = done(V.tensor_tensor(xy_2, xy_p, pn, ALU.mult))
            n_g = done(V.tensor_tensor(gain, unit, pn, ALU.mult))
            n_b = done(V.tensor_scalar(B, pn, -1.0, 1.0, ALU.mult, ALU.add))
            need(n)
            n_a = done(V.tensor_scalar(A, xy_2, y2, 1.0, ALU.add, ALU.add))
            need(n_b)
            n_b = done(V.scalar_tensor_tensor(out=B, in0=pn, scalar=1.0, in1=B, op0=ALU.add, op1=ALU.mult))
            n_d = done(V.scalar_tensor_tensor(out=den, in0=x2, scalar=y2, in1=xy_2, op0=ALU.mult, op1=ALU.add))
            need(n_a)
            done(V.tensor_tensor(Ap, A, pn, ALU.mult))
            need(n_b)
            n = done(V.tensor_tensor(xB, xy_2, B, ALU.mult))
            done(V.tensor_tensor(BB, B, B, ALU.mult))
            need(n_d)
            n_d = done(V.tensor_scalar(den, den, 1.0, MIN_NORM, ALU.add, ALU.max))
            need(n)
            done(V.tensor_tensor(xB, xB, A, ALU.mult))
            n = done(V.tensor_tensor(Ap, Ap, Ap, ALU.mult))
            need(n_d)
            done(V.reciprocal(rden, den))
            need(n)
            n = done(V.tensor_tensor(Ap, Ap, xB, ALU.add))
            done(V.tensor_tensor(alpha, A, gain, ALU.mult))
            need(n)
            done(V.scalar_tensor_tensor(out=num, in0=BB, scalar=y2, in1=Ap, op0=ALU.mult, op1=ALU.add))
            n = done(V.tensor_tensor(over, rden, rden, ALU.mult))
            n_e = done(V.tensor_scalar(beta, B, cb, None, ALU.mult))
            need(n)
            n = done(V.scalar_tensor_tensor(out=num, in0=num, scalar=0.0, in1=over, op0=ALU.max, op1=ALU.mult))
            need(n_e)
            done(V.tensor_tensor(alpha, alpha, rden, ALU.mult))
            done(V.tensor_tensor(beta, beta, rden, ALU.mult))
            done(V.reciprocal(rq, B))
            need(n)
            root(num, inv, root_tmp[:, 0, :], root_tmp[:, 1, :])
            n = done(V.tensor_tensor(zn, num, inv, ALU.mult))
            n_q = done(V.scalar_tensor_tensor(out=rq, in0=rq, scalar=inv_1_y2, in1=den, op0=ALU.mult, op1=ALU.mult))
            need(n)
            done(V.tensor_scalar(w2_, zn, MIN_NORM, BALL, ALU.max, ALU.min))
            n_z = done(V.tensor_scalar(zm, zn, MIN_NORM, None, ALU.max))
            need(n_q)
            n_q = done(V.tensor_scalar(rq, rq, BALL_RQ, None, ALU.min))
            need(n_q)

            def shrink():
                need(n_z)
                return rz, done(V.reciprocal(rz, zm))

            n = artanh_times(w2_, [
                lambda: done(V.scalar_tensor_tensor(out=ratio2, in0=w2_, scalar=1.0, in1=rq, op0=ALU.add, op1=ALU.mult)),
                lambda: done(V.scalar_tensor_tensor(out=ratio2, in0=w2_, scalar=1.0, in1=ratio2, op0=ALU.add, op1=ALU.mult), "ln2_in"),
            ], log2, 3, shrunk, 34, None, shrink)
            need(n)
            done(V.tensor_tensor(alpha, alpha, shrunk, ALU.mult))
            n = done(V.tensor_tensor(beta, beta, shrunk, ALU.mult), "end")
            need(n)

            bias_part = [tmp_a, tmp_b]

            def tangent_of(g):
                rows, n = slice(*GROUPS[g]), GROUPS[g][1] - GROUPS[g][0]
                V.tensor_tensor(bias_part[g % 2][:, 0:n, :], b0_row[:, None, :].broadcast_to([P, n, D]),
                                beta[:, rows, None].broadcast_to([P, n, D]), ALU.mult).then_inc(row_v, 1)
                need(ROW_END + g + 1)
                for t in range(n):
                    j = GROUPS[g][0] + t
                    i = V.scalar_tensor_tensor(out=h_rows[:, j, :], in0=h_rows[:, j, :], scalar=alpha[:, j:j + 1],
                                               in1=bias_part[g % 2][:, t, :], op0=ALU.mult, op1=ALU.add)
                i.then_inc(tangent, 1)

            def tangent_lo(f):
                rows = slice(*FEATS[f])
                dve.wait_ge(feat_hi_ready, f + 1)
                V.tensor_tensor(feat_lo[:, rows, :], h_rows[:, rows, :], feat_hi[:, rows, :].bitcast(F32),
                                ALU.subtract).then_inc(feat_lo_ready, 1)

            ROW_END = n
            assert ROW_END == ROW["end"], ROW_END
            tangent_of(0)
            tangent_of(1)
            for u in range(PLAIN, PAIRS):
                for g in TANGENT_BEFORE.get(u, []):
                    tangent_of(g)
                for f in FEAT_LO_BEFORE.get(u, []):
                    tangent_lo(f)
                split_lo(0, 0, u, first=(u < PLAIN + LO_BUFS))

            def post(b, step):
                v0, a0, g0 = (b - 1) * POST_V, (b - 1) * POST_A, (b - 1) * 2
                t0 = (b - 1) * BT

                def did(ins, count):
                    ins.then_inc(post_v, 1)

                if step == 2:
                    dve.wait_ge(post_g, g0 + 1)
                    did(V.tensor_scalar(s_kept, s_norm, MIN_NORM, None, ALU.max), 1)
                    did(V.tensor_scalar(s_ball, s_norm, ATANH_BALL, None, ALU.min), 2)
                    dve.wait_ge(post_v, v0 + 1)
                    did(V.reciprocal(inv_s, s_kept), 3)
                    dve.wait_ge(post_v, v0 + 3)
                    did(V.tensor_tensor(shrink_s, s_ball, inv_s, ALU.mult), 4)
                    dve.wait_ge(post_v, v0 + 4)
                    did(V.tensor_tensor(relu_t, shrink_s, relu_norm, ALU.mult), 5)
                    dve.wait_ge(post_v, v0 + 5)
                    did(V.tensor_scalar(tanh_in, relu_t, MIN_NORM, None, ALU.max), POSTV["tanh_in"])
                elif step == 3:
                    dve.wait_ge(post_v, v0 + 6)
                    did(V.reciprocal(inv_relu, tanh_in), 7)
                    dve.wait_ge(post_v, v0 + 7)
                    did(V.tensor_tensor(inv_relu, inv_relu, shrink_s, ALU.mult), 8)
                    dve.wait_ge(post_v, v0 + 8)
                    dve.wait_ge(post_a, a0 + POSTA["tanh"])
                    did(V.scalar_tensor_tensor(out=relu_gain, in0=relu_tanh, scalar=BALL, in1=inv_relu, op0=ALU.min, op1=ALU.mult), 9)
                    dve.wait_ge(post_v, v0 + 9)
                    for t in range(BT):
                        i = V.scalar_tensor_tensor(out=x_rows[:, t0 + t, :], in0=tmp_c[:, t, :], scalar=relu_gain[:, t:t + 1],
                                                   in1=x_rows[:, t0 + t, :], op0=ALU.mult, op1=ALU.add)
                    did(i, POSTV["x"])
                elif step == 4:
                    for t in range(BT):
                        i = V.bn_stats(bn6[:, t, :], x_rows[:, t0 + t, :])
                    did(i, POSTV["bn"])
                elif step == 5:
                    for t in range(BT):
                        i = V.bn_aggr(mv[:, t, :], bn6[:, t, :])
                    did(i, 12)
                    dve.wait_ge(post_v, v0 + 12)
                    did(V.tensor_scalar(post_var, mv[:, 0:BT, 1], LN_EPS, None, ALU.add), POSTV["var"])
                elif step == 6:
                    dve.wait_ge(post_g, g0 + 2)
                    did(V.scalar_tensor_tensor(out=post_shift, in0=mv[:, 0:BT, 0], scalar=-1.0, in1=post_rstd, op0=ALU.mult, op1=ALU.mult),
                        POSTV["shift"])

            def before_post(b, step):
                if step in (4, 5):
                    dve.wait_ge(post_v, (b - 1) * POST_V + POSTV[{4: "x", 5: "bn"}[step]])

            POST_AT = {7: 2, 8: 3, 10: 4, 12: 5, 13: 6}
            with dve.Fori(1, BLOCKS) as b:
                for u in range(PAIRS):
                    before_post(b, POST_AT.get(u))
                    split_lo(0, b, u)
                    if u in POST_AT:
                        post(b, POST_AT[u])

            def feat_split(f):
                first, end = FEATS1[f]
                dve.wait_ge(feat_hi_ready, len(FEATS) + f + 1)
                V.tensor_tensor(feat_lo[:, first:end, :], h_rows[:, first:end, :], feat_hi[:, first:end, :].bitcast(F32),
                                ALU.subtract).then_inc(feat_lo_ready, 1)

            for u in range(PAIRS):
                if u >= SPLIT_KEPT:
                    split_lo(1, 0, u)
                for step in KEPT_POST_DVE.get(u, []):
                    before_post(BLOCKS, step)
                    post(BLOCKS, step)
                for f in KEPT_FEAT_DVE.get(u, []):
                    feat_split(f)

            def last(b, step):
                v0 = (b - 1) * LAST_V
                rows = bass.ds(b * -BT + TILES, BT)
                if step == 0:
                    V.tensor_copy(tmp_c[:, :, :], h_rows[:, rows, :]).then_inc(last_v, 1)
                else:
                    finish(range(BT), rows, b, v0 + 2)

            def finish(tiles, rows, products, step):
                tiles = slice(tiles[0], tiles[-1] + 1)
                y = tmp_c[:, tiles, :]
                dve.wait_ge(last_p, products)
                V.tensor_tensor(y, prod.rearrange("p (t d) -> p t d", d=D)[:, tiles, :],
                                b1_row[:, None, :].broadcast_to(list(y.shape)), ALU.add).then_inc(last_v, 1)
                dve.wait_ge(last_v, step)
                V.scalar_tensor_tensor(out=y.rearrange("p t d -> p (t d)"), in0=y.rearrange("p t d -> p (t d)"), scalar=0.0,
                                       in1=x_rows[:, rows, :].rearrange("p t d -> p (t d)"),
                                       op0=ALU.max, op1=ALU.add).then_inc(last_v, 1)

            def layer1_block(b, final=False):
                for u in range(PAIRS):
                    split_lo(1, b, u)
                    if u == 1:
                        last(b, 0)
                    if u == 8:
                        last(b, 1)
                    if final and u == PAIRS - 3:
                        dve.wait_ge(stored, b * 16)
                        last(BLOCKS, 0)
                if not final:
                    dve.wait_ge(stored, b * 16)

            with dve.Fori(1, BLOCKS - 1) as b:
                layer1_block(b)
            layer1_block(BLOCKS - 1, final=True)
            for h in range(HALVES):
                tiles = range(h * HALF, (h + 1) * HALF)
                finish(tiles, slice(tiles[0], tiles[-1] + 1), BLOCKS + h, (BLOCKS - 1) * LAST_V + LASTV["h"] + 2 * h + 1)


ROW = {"bn0": 1, "bn1": 2, "bn2": 3, "bn3": 4, "aggr": 5, "var": 6, "sums": 7, "ln1_in": 27, "tanh_in": 37,
       "ln2_in": 82, "end": 94}
POSTV = {"tanh_in": 6, "x": 10, "bn": 11, "var": 13, "shift": 14}
POSTA = {"sums": 3, "tanh": 4}
POST_V, POST_A = 14, 5
LASTV = {"h": 1, "y": 3}
LAST_V = 3
GROUPS = [(16, 18), (18, 24), (24, 32), (0, 8), (8, 16)]
FEATS = [(24, 32), (0, 8), (8, 16), (16, 24)]
FEAT_TANGENTS = [3, 4, 5, 2]
PRE_SPLIT = 2
TANGENT_BEFORE = {4: [2], 7: [3], 9: [4]}
FEAT_LO_BEFORE = {5: [0], 8: [1], 11: [2], 13: [3]}
FEAT_AT = {8: 0, 9: 1, 11: 2, 13: 3}
FEATS1 = [(0, 8), (8, 12), (12, 16), (16, 24), (24, 32)]
KEPT_H_AT = 0
KEPT_POST_ACT = {2: [0], 3: [1, 2], 4: [3], 7: [4], 11: [5]}
KEPT_FEAT_ACT = {0: [0], 1: [1], 2: [2], 5: [3], 11: [4]}
KEPT_POST_DVE = {4: [2], 5: [3], 6: [4, 5], 7: [6]}
KEPT_FEAT_DVE = {0: [0], 1: [1], 3: [2], 6: [3], 10: [4]}


def kernel(x, adj, L0_gnn_weight, L0_gnn_bias, L1_gnn_weight, L1_gnn_bias):
    import concourse.bacc as bacc
    from concourse.bass_utils import run_bass_kernel_spmd

    x, adj, w0, w1 = (np.ascontiguousarray(a) for a in (x, adj, L0_gnn_weight, L1_gnn_weight))
    units = adj.reshape(BLOCKS, BLOCK, PAIRS, 2, P).transpose(0, 2, 4, 3, 1)
    units = np.ascontiguousarray(units).reshape(LAYER_UNITS, P, UNIT)
    eye = np.eye(D, dtype=np.float32)
    center = eye - np.float32(1.0 / D)
    consts = np.ascontiguousarray(np.stack([w0.T, w0, w1[:D], w1[D:], eye, center], axis=1))
    arrays = {
        "x": x, "x_t": np.ascontiguousarray(x.T), "adj_units": units, "consts": consts,
        "bias0": np.ascontiguousarray(L0_gnn_bias), "bias1": np.ascontiguousarray(L1_gnn_bias),
    }
    nc = bacc.Bacc("TRN2", target_bir_lowering=False, num_devices=1, dynamic_dma_scratch_size=1024)
    args = [nc.dram_tensor(k, a.shape, mybir.dt.from_np(a.dtype), kind="ExternalInput").ap() for k, a in arrays.items()]
    args.append(nc.dram_tensor("out", (N, D), F32, kind="ExternalOutput").ap())
    two_layers(nc, *args)
    got = run_bass_kernel_spmd(nc, [arrays], core_ids=[0])
    return got.results[0]["out"]
```
